# Optimizing a Trainium2 kernel written in Bass

```python
import numpy as np
import jax
import jax.numpy as jnp

def _softmax(x, axis=-1):
    return jax.nn.softmax(x, axis=axis)

def _gelu(x):
    return jax.nn.gelu(x, approximate=True)

def _silu(x):
    return jax.nn.silu(x)

def _sigmoid(x):
    return jax.nn.sigmoid(x)

def _layernorm(x, axis=-1, eps=1e-05):
    m = jnp.mean(x, axis=axis, keepdims=True)
    v = jnp.var(x, axis=axis, keepdims=True)
    return (x - m) / jnp.sqrt(v + eps)

def _scatter_add(tgt, idx, src, axis=0):
    return tgt.at[idx].add(src)

def _segment_sum(src, seg, n):
    return jax.ops.segment_sum(src, seg, n)
kernel_name = 'mk_gnn_resnorm_d1_gnn_r32_4e9b6c'

def setup_inputs(seed: int=0):
    np.random.seed(seed)
    _w = jnp.asarray

    def _rec_inputs():
        import jax
        import jax.numpy as jnp
        _gk = jax.random.key(seed)
        x = -0.000202 + 1 * jax.random.normal(jax.random.fold_in(_gk, 1), (3125, 128), jnp.float32)
        _s = jax.random.randint(jax.random.fold_in(_gk, 2), (25000,), 0, 3125, jnp.int32)
        _d = jax.random.randint(jax.random.fold_in(_gk, 3), (25000,), 0, 3125, jnp.int32)
        _loop = jnp.arange(3125, dtype=jnp.int32)
        src = jnp.concatenate([_s, _d, _loop])
        dst = jnp.concatenate([_d, _s, _loop])
        _o = jnp.argsort(dst, stable=True)
        src = src[_o]
        dst = dst[_o]
        edge_attr_128 = -8.513e-05 + 0.999844 * jax.random.normal(jax.random.fold_in(_gk, 12), (53125, 128), jnp.float32)
        return (x, src, dst, edge_attr_128)
    x, src, dst, edge_attr_128 = _rec_inputs()

    def _L0_gnn_setup():
        import jax, jax.numpy as jnp
        import numpy as np
        N_NODES = 50000
        N_EDGES = 20000
        EMB = 128
        BN_EPS = 1e-05
        key = jax.random.key(seed)
        ks = jax.random.split(key, 8)
        node_feat = jax.random.normal(ks[0], (N_NODES, EMB), dtype=jnp.float32)
        edge_feat = jax.random.normal(ks[1], (N_EDGES, EMB), dtype=jnp.float32)
        src = jax.random.randint(ks[2], (N_EDGES,), 0, N_NODES, dtype=jnp.int64)
        dst = jax.random.randint(ks[3], (N_EDGES,), 0, N_NODES, dtype=jnp.int64)
        eps = jnp.zeros((1,), dtype=jnp.float32)
        W1 = jax.random.normal(ks[4], (EMB, 2 * EMB), dtype=jnp.float32) * (1.0 / np.sqrt(EMB))
        b1 = jnp.zeros((2 * EMB,), dtype=jnp.float32)
        gamma = jnp.ones((2 * EMB,), dtype=jnp.float32)
        beta = jnp.zeros((2 * EMB,), dtype=jnp.float32)
        W2 = jax.random.normal(ks[5], (2 * EMB, EMB), dtype=jnp.float32) * (1.0 / np.sqrt(2 * EMB))
        b2 = jnp.zeros((EMB,), dtype=jnp.float32)
        return {'node_feat': node_feat, 'edge_feat': edge_feat, 'src': src, 'dst': dst, 'eps': eps, 'W1': W1, 'b1': b1, 'gamma': gamma, 'beta': beta, 'W2': W2, 'b2': b2}
    _L0_gnn_all = _L0_gnn_setup()
    _L0_gnn_in = {k: v for k, v in _L0_gnn_all.items() if k in ('eps', 'W1', 'b1', 'gamma', 'beta', 'W2', 'b2')}
    del _L0_gnn_all
    return {'x': x, 'src': src, 'dst': dst, 'edge_attr_128': edge_attr_128, 'L0_gnn_eps': _L0_gnn_in['eps'], 'L0_gnn_W1': _L0_gnn_in['W1'], 'L0_gnn_b1': _L0_gnn_in['b1'], 'L0_gnn_gamma': _L0_gnn_in['gamma'], 'L0_gnn_beta': _L0_gnn_in['beta'], 'L0_gnn_W2': _L0_gnn_in['W2'], 'L0_gnn_b2': _L0_gnn_in['b2']}

def reference(x, src, dst, edge_attr_128, L0_gnn_eps, L0_gnn_W1, L0_gnn_b1, L0_gnn_gamma, L0_gnn_beta, L0_gnn_W2, L0_gnn_b2):
    import jax
    import jax.numpy as jnp

    def _L0_gnn_ref(node_feat, edge_feat, src, dst, eps, W1, b1, gamma, beta, W2, b2):
        import jax, jax.numpy as jnp
        import numpy as np
        N_NODES = 50000
        N_EDGES = 20000
        EMB = 128
        BN_EPS = 1e-05
        msg = node_feat[src] + edge_feat
        neigh = jax.ops.segment_sum(msg, dst, num_segments=node_feat.shape[0])
        rst = (1.0 + eps[0]) * node_feat + neigh
        h = rst @ W1 + b1
        mean = jnp.mean(h, axis=0)
        var = jnp.var(h, axis=0)
        h = (h - mean) * jax.lax.rsqrt(var + BN_EPS) * gamma + beta
        h = jax.nn.relu(h)
        out = h @ W2 + b2
        return out
    x = _layernorm(x + _L0_gnn_ref(x, edge_attr_128, src, dst, L0_gnn_eps, L0_gnn_W1, L0_gnn_b1, L0_gnn_gamma, L0_gnn_beta, L0_gnn_W2, L0_gnn_b2), axis=-1)
    return x

_drawn_inputs = setup_inputs


def setup_inputs(seed=0):
    import zlib

    import numpy as np

    out = dict(_drawn_inputs(seed))
    spreads = {'L0_gnn_b1': (0.0, 0.1),
     'L0_gnn_gamma': (1.0, 0.2),
     'L0_gnn_beta': (0.0, 0.1),
     'L0_gnn_b2': (0.0, 0.1)}
    factors = {}
    for name, (base, spread) in spreads.items():
        noise = np.random.default_rng([zlib.crc32(name.encode()), seed]).standard_normal(out[name].shape)
        drawn = base * np.exp(spread * noise) if base else spread * noise
        out[name] = jnp.asarray(drawn.astype(out[name].dtype))
    for name, factor in factors.items():
        out[name] = (out[name] * factor).astype(out[name].dtype)
    return out
```

```python
from contextlib import ExitStack

import concourse.bass as bass
from concourse import mybir

ALU = mybir.AluOpType
ACT = mybir.ActivationFunctionType
AX_X = mybir.AxisListType.X
F32 = mybir.dt.float32
I32 = mybir.dt.int32

P = 128
BANK = 512
LN_EPS = 1e-5
BN_EPS = 1e-5
ROWS = 2
GROUP = P * ROWS
WIN = 20
CHUNK = 4
BODY = 8
PAD = 8192


def gnn_layer(nc, x, src, dst, edge, eps, w1, b1, gamma, beta, w2, b2, out):
    N, D = x.shape
    E = src.shape[0]
    H = w1.shape[1]
    HH = H // P
    NT = -(-N // P)
    NL = N - (NT - 1) * P
    NB = -(-N // BANK)
    Q = -(-E // (2 * GROUP))
    QW = 2 * GROUP
    QL = E - (Q - 1) * QW
    G = 2 * Q
    GL = E - (G - 1) * GROUP
    C = G // CHUNK
    T = G * ROWS
    STEPS = G // BODY
    assert D == P and H == HH * P and G % BODY == 0 and GL > 0 and Q <= P and 4 * Q <= BANK and QW - QL <= GL
    HJ = 2 * ROWS

    def width(b):
        return min(BANK, N - b * BANK)

    def rows_of(t):
        return NL if t == NT - 1 else P

    x_main = x[0:(NT - 1) * P, :].rearrange("(t p) d -> p t d", p=P)
    out_v = out[0:(NT - 1) * P, :].rearrange("(t p) d -> p t d", p=P)

    with ExitStack() as ctx:
        def sb(name, shape, dt=F32):
            return ctx.enter_context(nc.sbuf_tensor(name, shape, dt))

        def sem(name):
            return ctx.enter_context(nc.semaphore(name))

        xN = sb("xN", [P, NT, D])
        aggT = sb("aggT", [P, N + WIN])
        hT = sb("hT", [P, HH, N])
        yN = sb("yN", [P, NT, D])
        oN = sb("oN", [P, NT, D])
        w1_sb = sb("w1_sb", [P, H])
        w2_sb = sb("w2_sb", [P, HH, D])
        col = sb("col", [P, 3, HH])
        row = sb("row", [1, D + 1])
        ones = sb("ones", [P, P])
        diff = sb("diff", [P, P])
        ident = sb("ident", [P, P])
        iota_w = sb("iota_w", [P, CHUNK * ROWS, WIN])
        iota_b = sb("iota_b", [P, BANK])
        b2e = sb("b2e", [P, D + 1])
        srcq = sb("srcq", [Q, QW], I32)
        dstq = sb("dstq", [Q, QW], I32)
        srcf = sb("srcf", [Q, QW])
        dstf = sb("dstf", [Q, QW])
        dstm = sb("dstm", [Q, QW])
        ends = sb("ends", [Q, 4])
        endd = sb("endd", [Q, 4, Q])
        low = sb("low", [P, Q, 2])
        high = sb("high", [P, Q, 2])
        lowi = sb("lowi", [P, Q, 2], I32)
        span = sb("span", [P, 4])
        wide = sb("wide", [P, 1], I32)
        dcol = sb("dcol", [P, Q, HJ])
        rel = sb("rel", [P, T + CHUNK * ROWS])
        srci = sb("srci", [P, Q, HJ], I32)
        idx = sb("idx", [P, 2, CHUNK * ROWS], I32)
        ebuf = sb("ebuf", [P, 2, CHUNK, ROWS * D])
        gbuf = sb("gbuf", [P, BODY, ROWS, D])
        hit = sb("hit", [P, 2, CHUNK * ROWS, WIN])
        msg = sb("msg", [P, ROWS, D])
        hit_all = sb("hit_all", [P, NB, BANK])
        bst = sb("bst", [P, HH, NB, 6])
        bag = sb("bag", [P, HH, 2])
        sd = sb("sd", [P, HH])
        rsd = sb("rsd", [P, HH])
        scl = sb("scl", [P, HH])
        ms = sb("ms", [P, HH])
        sft = sb("sft", [P, HH])
        epsc = sb("epsc", [P, 2])
        rl = sb("rl", [P, 2, BANK])
        lst = sb("lst", [P, NT, 6])
        lag = sb("lag", [P, NT, 2])
        lsd = sb("lsd", [P, NT])
        lrs = sb("lrs", [P, NT])
        lnb = sb("lnb", [P, NT])
        warm = sb("warm", [1, 1])

        ps = ctx.enter_context(nc.psum_tensor("ps", [P, 8, BANK], F32))

        s_idx = sem("s_idx")
        s_idx1 = sem("s_idx1")
        s_fill = sem("s_fill")
        s_x = sem("s_x")
        s_w = sem("s_w")
        s_edge = [sem(f"s_edge{i}") for i in range(2)]
        s_tail = sem("s_tail")
        s_gat = [sem(f"s_gat{i}") for i in range(BODY)]
        s_cst = sem("s_cst")
        s_id = sem("s_id")
        s_pad = sem("s_pad")
        s_q = sem("s_q")
        s_end = sem("s_end")
        s_endd = sem("s_endd")
        s_bc = sem("s_bc")
        s_turn = sem("s_turn")
        s_b2e = sem("s_b2e")
        s_e1 = sem("s_e1")
        s_low = sem("s_low")
        s_dc = sem("s_dc")
        s_rel = sem("s_rel")
        s_srci = sem("s_srci")
        s_flag = sem("s_flag")
        s_xt = sem("s_xt")
        s_xs = sem("s_xs")
        s_xb = sem("s_xb")
        s_ix = sem("s_ix")
        s_hit = sem("s_hit")
        s_win = sem("s_win")
        s_acc = sem("s_acc")
        s_agg = sem("s_agg")
        s_ge = sem("s_ge")
        s_go = sem("s_go")
        s_gg = sem("s_gg")
        s_gx = sem("s_gx")
        s_gm = sem("s_gm")
        s_gh = sem("s_gh")
        s_gp = sem("s_gp")
        s_gz = sem("s_gz")
        s_h = sem("s_h")
        s_hc = sem("s_hc")
        s_bn = sem("s_bn")
        s_sd = sem("s_sd")
        s_sc = sem("s_sc")
        s_ra = sem("s_ra")
        s_rv = sem("s_rv")
        s_r0 = sem("s_r0")
        s_y = sem("s_y")
        s_yc = sem("s_yc")
        s_lg = sem("s_lg")
        s_lt = sem("s_lt")
        s_ls = sem("s_ls")
        s_lr = sem("s_lr")
        s_ln = sem("s_ln")
        s_o = sem("s_o")
        s_out = sem("s_out")

        block = ctx.enter_context(nc.Block())
        GX = 7
        edge_g = edge[0:(G - 1) * GROUP, :].rearrange("(g p j) d -> p g (j d)", p=P, j=ROWS)
        tail_r = GL // ROWS
        tail_v = edge[(G - 1) * GROUP:(G - 1) * GROUP + tail_r * ROWS, :].rearrange("(p j) d -> p (j d)", j=ROWS)
        tail_1 = edge[E - 1:E, :]

        @block.sync
        def _(sp):
            sp.dma_start(dstq[0:Q - 1, :], dst[0:(Q - 1) * QW].rearrange("(q c) -> q c", c=QW)).then_inc(s_idx, 16)
            sp.dma_start(dstq[Q - 1:Q, 0:QL], dst[(Q - 1) * QW:E].unsqueeze(0)).then_inc(s_idx, 16)
            sp.dma_start(dstq[Q - 1:Q, QL:QW], dst[E - (QW - QL):E].unsqueeze(0)).then_inc(s_idx, 16)
            sp.wait_ge(s_pad, 1)
            sp.dma_start(srcq[0:Q - 1, :], src[0:(Q - 1) * QW].rearrange("(q c) -> q c", c=QW)).then_inc(s_idx1, 16)
            sp.dma_start(srcq[Q - 1:Q, 0:QL], src[(Q - 1) * QW:E].unsqueeze(0)).then_inc(s_idx1, 16)
            sp.wait_ge(s_flag, 1)
            flag = sp.value_load(wide[0:1, 0:1], min_val=0, max_val=1)
            with sp.If(flag != 0):
                def group(g):
                    sp.dma_start(ebuf[:, 0, 0, :], edge_g[:, g, :]).then_inc(s_ge, 16)
                group(0)
                with sp.Fori(1, G - 1) as g:
                    sp.wait_ge(s_gm, g * 2)
                    group(g)
                sp.wait_ge(s_gm, (G - 1) * 2)
                sp.dma_start(ebuf[tail_r:tail_r + 1, 0, 0, 0:D], tail_1).then_inc(s_tail, 16)
                sp.wait_ge(s_tail, 16)
                sp.dma_start(ebuf[0:tail_r, 0, 0, :], tail_v).then_inc(s_ge, 16)
            with sp.Else():
                def chunk(c, k):
                    sp.dma_start(ebuf[:, k, :, :], edge_g[:, bass.ds(c * CHUNK, CHUNK), :]).then_inc(s_edge[k], 16)
                chunk(0, 0)
                chunk(1, 1)
                with sp.Fori(1, STEPS - 1) as i:
                    for k in range(2):
                        sp.wait_ge(s_win, i * BODY + (k + 1) * CHUNK - BODY)
                        chunk(i * 2 + k, k)
                sp.wait_ge(s_win, (C - 3) * CHUNK)
                chunk(C - 2, 0)
                sp.wait_ge(s_win, (C - 2) * CHUNK)
                sp.dma_start(ebuf[tail_r:tail_r + 1, 1, CHUNK - 1, 0:D], tail_1).then_inc(s_tail, 16)
                sp.dma_start(ebuf[0:tail_r, 1, CHUNK - 1, :], tail_v).then_inc(s_tail, 16)
                sp.wait_ge(s_tail, 32)
                sp.dma_start(ebuf[:, 1, 0:CHUNK - 1, :],
                             edge_g[:, (C - 1) * CHUNK:G - 1, :]).then_inc(s_edge[1], 16)

        @block.gpsimd
        def _(pool):
            nc.gpsimd.iota(diff[:, :], [[1, P]], base=0, channel_multiplier=-1,
                           allow_small_or_imprecise_dtypes=True).then_inc(s_cst, 1)
            nc.gpsimd.memset(ones[:, :], 1.0).then_inc(s_cst, 1)
            nc.gpsimd.iota(iota_w[:, :, :], [[0, CHUNK * ROWS], [1, WIN]], base=0, channel_multiplier=0,
                           allow_small_or_imprecise_dtypes=True).then_inc(s_cst, 1)
            nc.gpsimd.iota(iota_b[:, :], [[1, BANK]], base=0, channel_multiplier=0,
                           allow_small_or_imprecise_dtypes=True).then_inc(s_cst, 1)
            pool.wait_ge(s_flag, 1)
            flag = pool.value_load(wide[0:1, 0:1], min_val=0, max_val=1)
            src_c = srci[:, :, :].rearrange("p q k -> p (q k)")

            def gather(to, ix):
                pool.sem_inc(s_go, 1)
                return nc.gpsimd.indirect_dma_start(to, None, x[:, :], bass.IndirectOffsetOnAxis(ap=ix, axis=0))

            with pool.If(flag != 0):
                with pool.Fori(0, G) as g:
                    pool.wait_ge(s_gm, g * 2)
                    nc.gpsimd.tensor_copy(idx[:, 0, 0:ROWS], src_c[:, bass.ds(g * ROWS, ROWS)]).then_inc(s_gx, 1)
                    pool.wait_ge(s_gx, g + 1)
                    for j in range(ROWS):
                        gather(gbuf[:, 0, j, :], idx[:, 0, j:j + 1]).then_inc(s_gg, 16)
                    pool.wait_ge(s_gg, g * 32 + 32)
            with pool.Else():
                def body(i, first):
                    for a in range(2):
                        if not first:
                            for k in range(a * CHUNK, (a + 1) * CHUNK):
                                pool.wait_ge(s_gat[k], i * (16 * ROWS))
                        nc.gpsimd.tensor_copy(idx[:, a, :], src_c[:, bass.ds(i * (BODY * ROWS) + a * CHUNK * ROWS, CHUNK * ROWS)]).then_inc(s_ix, 1)
                        pool.wait_ge(s_ix, i * 2 + a + 1)
                        for k in range(a * CHUNK, (a + 1) * CHUNK):
                            if not first:
                                pool.wait_ge(s_win, i * BODY + (k + 1 - BODY))
                            for j in range(ROWS):
                                gather(gbuf[:, k, j, :],
                                       idx[:, a, (k - a * CHUNK) * ROWS + j:(k - a * CHUNK) * ROWS + j + 1]).then_inc(s_gat[k], 16)
                body(0, True)
                with pool.Fori(1, STEPS) as i:
                    body(i, False)

        @block.scalar
        def _(act):
            act.dma_start(xN[:, 0:NT - 1, :], x_main).then_inc(s_x, 16)
            act.dma_start(xN[0:NL, NT - 1, :], x[(NT - 1) * P:N, :]).then_inc(s_x, 16)
            act.dma_start(row[0:1, 0:D], b2.unsqueeze(0)).then_inc(s_w, 16)
            act.dma_start(row[0:1, D:D + 1], eps.unsqueeze(0)).then_inc(s_w, 16)
            act.dma_start(w1_sb[:, :], w1).then_inc(s_w, 16)
            act.dma_start(w2_sb[:, :, :], w2.rearrange("(h p) d -> p h d", p=P)).then_inc(s_w, 16)
            for k, v in enumerate((b1, gamma, beta)):
                act.dma_start(col[:, k, :], v.rearrange("(h p) -> p h", p=P),
                              allow_slow_non_contiguous=True).then_inc(s_w, 16)
            act.wait_ge(s_cst, 2)
            nc.scalar.activation(warm[0:1, 0:1], ones[0:1, 0:1], ACT.Sqrt).then_inc(s_r0, 1)
            act.wait_ge(s_e1, 2)
            for b in range(NB):
                act.wait_ge(s_xt, b + 1)
                nc.scalar.activation(aggT[:, b * BANK:b * BANK + width(b)], ps[:, b % 2, 0:width(b)], ACT.Copy,
                                     scale=b2e[:, D:D + 1]).then_inc(s_xs, 1)
            for b in range(NB):
                for h in range(HH):
                    n = b * HH + h
                    act.wait_ge(s_h, n + 1)
                    nc.scalar.activation(hT[:, h, b * BANK:b * BANK + width(b)], ps[:, n % 4, 0:width(b)],
                                         ACT.Identity, bias=col[:, 0, h:h + 1]).then_inc(s_hc, 1)
            act.wait_ge(s_bn, 2 * HH)
            nc.scalar.activation(sd[:, :], bag[:, :, 1], ACT.Sqrt, bias=epsc[:, 0:1]).then_inc(s_sd, 1)
            act.wait_ge(s_sc, 4)
            for b in range(NB):
                hb = hT[:, 0, b * BANK:b * BANK + width(b)]
                nc.scalar.activation(hb, hb, ACT.Relu, scale=scl[:, 0:1], bias=sft[:, 0:1]).then_inc(s_ra, 1)
            for b in range(NB):
                t0, t1 = 4 * b, min(4 * b + 4, NT)
                act.wait_ge(s_lg, t1)
                r = rows_of(t1 - 1)
                nc.scalar.activation(lsd[0:r, t0:t1], lag[0:r, t0:t1, 1], ACT.Sqrt,
                                     bias=epsc[0:r, 1:2]).then_inc(s_ls, 1)
                act.wait_ge(s_ln, b + 1)
                for t in range(t0, t1):
                    last = nc.scalar.activation(oN[0:rows_of(t), t, :], yN[0:rows_of(t), t, :], ACT.Identity,
                                                scale=lrs[0:rows_of(t), t:t + 1], bias=lnb[0:rows_of(t), t:t + 1])
                    last.then_inc(s_o, 1)
                act.wait_ge(s_o, t1)
                if t1 < NT:
                    act.dma_start(out_v[:, t0:t1, :], oN[:, t0:t1, :]).then_inc(s_out, 16)
                else:
                    act.dma_start(out[(NT - 1) * P:N, :], oN[0:NL, NT - 1, :]).then_inc(s_out, 16)
            assert NT == 4 * (NB - 1) + 1
            act.wait_ge(s_out, 16 * NB)

        @block.tensor
        def _(pe):
            pe.wait_ge(s_cst, 2)
            pe.wait_ge(s_w, 112)
            nc.tensor.matmul(ps[:, 6, 0:D + 1], ones[0:1, :], row[0:1, :], start=True, stop=True).then_inc(s_b2e, 1)
            pe.wait_ge(s_endd, 4)
            nc.tensor.matmul(ps[:, 2, 0:4 * Q], ones[0:Q, :], endd[:, :, :].rearrange("q k r -> q (k r)"),
                             start=True, stop=True).then_inc(s_bc, 1)
            pe.wait_ge(s_id, 1)
            pe.wait_ge(s_q, 5)
            for n, a in enumerate((dstm, srcf)):
                v = a[:, :].rearrange("q (h p j) -> q h j p", h=2, j=ROWS)
                for k in range(HJ):
                    last = nc.tensor.transpose(ps[:, 3 + n, k * Q:(k + 1) * Q], v[:, k // ROWS, k % ROWS, :],
                                               ident[0:Q, 0:Q])
                last.then_inc(s_turn, 1)
            pe.wait_ge(s_x, 32)
            for b in range(NB):
                if b >= 2:
                    pe.wait_ge(s_xs, b - 1)
                for t in range(4 * b, min(4 * b + 4, NT)):
                    r = rows_of(t)
                    k = (t - 4 * b) * P
                    last = nc.tensor.transpose(ps[:, b % 2, k:k + r], xN[0:r, t, :], ident[0:r, 0:r])
                last.then_inc(s_xt, 1)
            pe.wait_ge(s_flag, 1)
            flag = pe.value_load(wide[0:1, 0:1], min_val=0, max_val=1)
            with pe.If(flag != 0):
                pe.wait_ge(s_xs, NB)
                pe.wait_ge(s_gz, 1)
                pe.wait_ge(s_rel, 3)
                for b in range(NB):
                    last = nc.tensor.matmul(ps[:, b, :], msg[:, 0, :], iota_b[:, :], start=True, stop=False,
                                            skip_group_check=True)
                last.then_inc(s_gp, 1)
                with pe.Fori(0, G) as g:
                    for j in range(ROWS):
                        pe.wait_ge(s_gh, g * ROWS + j + 1)
                        for b in range(NB):
                            last = nc.tensor.matmul(ps[:, b, :], msg[:, j, :], hit_all[:, b, :], start=False,
                                                    stop=False, skip_group_check=True)
                        last.then_inc(s_gp, 1)
                for b in range(NB):
                    last = nc.tensor.matmul(ps[:, b, :], msg[:, 0, :], iota_b[:, :], start=False, stop=True,
                                            skip_group_check=True)
                last.then_inc(s_gp, 1)
            with pe.Else():
                with pe.Fori(0, STEPS) as i:
                    for k in range(BODY):
                        a = k // CHUNK
                        if k % CHUNK == 0:
                            pe.wait_ge(s_hit, i * 2 + (a + 1))
                            pe.wait_ge(s_edge[a], i * 16 + 16)
                        pe.wait_ge(s_acc, i * BODY + (k + 4))
                        pe.wait_ge(s_gat[k], i * (16 * ROWS) + 16 * ROWS)
                        w = ps[:, 4 + k % 4, 0:WIN]
                        for j in range(ROWS):
                            u = (k % CHUNK) * ROWS + j
                            nc.tensor.matmul(w, ebuf[:, a, k % CHUNK, j * D:(j + 1) * D], hit[:, a, u, :],
                                             start=(j == 0), stop=False)
                            last = nc.tensor.matmul(w, gbuf[:, k, j, :], hit[:, a, u, :],
                                                    start=False, stop=(j == ROWS - 1))
                        last.then_inc(s_win, 1)
            for b in range(NB):
                pe.wait_ge(s_agg, b + 1)
                for h in range(HH):
                    n = b * HH + h
                    if n >= 4:
                        pe.wait_ge(s_hc, n - 3)
                    nc.tensor.matmul(ps[:, n % 4, 0:width(b)], w1_sb[:, h * P:(h + 1) * P],
                                     aggT[:, b * BANK:b * BANK + width(b)], start=True, stop=True).then_inc(s_h, 1)
            for b in range(NB):
                pe.wait_ge(s_ra, b + 1)
                pe.wait_ge(s_rv, b + 1)
                if b < 4:
                    pe.wait_ge(s_hc, NB * HH)
                if b >= 4:
                    pe.wait_ge(s_yc, b - 3)
                for t in range(4 * b, min(4 * b + 4, NT)):
                    r = rows_of(t)
                    k = (t - 4 * b) * P
                    for h in range(HH):
                        last = nc.tensor.matmul(ps[0:r, b % 4, k:k + D], hT[:, h, t * P:t * P + r], w2_sb[:, h, :],
                                                start=(h == 0), stop=(h == HH - 1))
                last.then_inc(s_y, 1)

        @block.vector
        def _(dve):
            nc.vector.memset(srcq[:, :], -1).then_inc(s_pad, 1)
            dve.wait_ge(s_cst, 4)
            nc.vector.tensor_scalar(ident[:, :], diff[:, :], 0.0, None, ALU.is_equal).then_inc(s_id, 1)
            nc.vector.memset(rel[:, T:T + CHUNK * ROWS], -1.0).then_inc(s_rel, 1)
            nc.vector.memset(epsc[:, 0:1], BN_EPS).then_inc(s_id, 1)
            nc.vector.memset(epsc[:, 1:2], LN_EPS).then_inc(s_id, 1)
            nc.vector.memset(aggT[:, N:N + WIN], 0.0).then_inc(s_id, 1)
            dve.wait_ge(s_idx, 48)
            nc.vector.tensor_copy(dstf[:, :], dstq[:, :]).then_inc(s_q, 1)
            dve.wait_ge(s_q, 1)
            dv = dstf[:, :].rearrange("q (h c) -> q h c", h=2)
            nc.vector.tensor_reduce(ends[:, 0:2], dv, AX_X, ALU.min).then_inc(s_end, 1)
            nc.vector.tensor_reduce(ends[:, 2:4], dv, AX_X, ALU.max).then_inc(s_end, 1)
            dve.wait_ge(s_end, 2)
            dve.wait_ge(s_id, 4)
            for k in range(4):
                nc.vector.tensor_scalar(endd[:, k, :], ident[0:Q, 0:Q], ends[:, k:k + 1], None,
                                        ALU.mult).then_inc(s_endd, 1)
            dve.wait_ge(s_idx1, 32)
            dve.wait_ge(s_pad, 1)
            nc.vector.tensor_copy(srcf[:, :], srcq[:, :]).then_inc(s_q, 1)
            dve.wait_ge(s_q, 2)
            nc.vector.tensor_scalar(dstm[:, :], srcf[:, :], 0.0, float(PAD), ALU.min, ALU.mult).then_inc(s_q, 1)
            dve.wait_ge(s_q, 3)
            nc.vector.tensor_tensor(dstm[:, :], dstm[:, :], dstf[:, :], ALU.add).then_inc(s_q, 1)
            nc.vector.tensor_scalar(srcf[:, :], srcf[:, :], 0.0, None, ALU.max).then_inc(s_q, 1)
            dve.wait_ge(s_bc, 1)
            bc = ps[:, 2, 0:4 * Q].rearrange("p (k h q) -> p k q h", k=2, h=2)
            nc.vector.tensor_copy(low[:, :, :], bc[:, 0, :, :]).then_inc(s_low, 1)
            nc.vector.tensor_copy(high[:, :, :], bc[:, 1, :, :]).then_inc(s_low, 1)
            dve.wait_ge(s_low, 2)
            nc.vector.tensor_copy(lowi[:, :, :], low[:, :, :]).then_inc(s_low, 1)
            nc.vector.tensor_tensor(high[:, :, :], high[:, :, :], low[:, :, :], ALU.subtract).then_inc(s_low, 1)
            dve.wait_ge(s_low, 4)
            nc.vector.tensor_reduce(span[:, 0:1], high[:, :, :].rearrange("p q h -> p (q h)"), AX_X,
                                    ALU.max).then_inc(s_low, 1)
            dve.wait_ge(s_turn, 1)
            nc.vector.tensor_copy(dcol[:, :, :], ps[:, 3, 0:T].rearrange("p (k q) -> p q k", q=Q)).then_inc(s_dc, 1)
            dve.wait_ge(s_dc, 1)
            rel_v = rel[:, 0:T].rearrange("p (g j) -> p g j", j=ROWS)
            nc.vector.tensor_tensor(rel_v, dcol[:, :, :].rearrange("p q (h j) -> p (q h) j", j=ROWS),
                                    low[:, :, :].rearrange("p q h -> p (q h)").unsqueeze(2).to_broadcast([P, G, ROWS]),
                                    ALU.subtract).then_inc(s_rel, 1)
            dve.wait_ge(s_turn, 2)
            nc.vector.tensor_copy(srci[:, :, :], ps[:, 4, 0:T].rearrange("p (k q) -> p q k", q=Q)).then_inc(s_rel, 1)
            dve.wait_ge(s_low, 5)
            nc.vector.tensor_scalar(wide[:, :], span[:, 0:1], float(WIN), None, ALU.is_ge).then_inc(s_srci, 1)
            dve.wait_ge(s_rel, 3)
            dve.wait_ge(s_srci, 1)
            dve.wait_ge(s_b2e, 1)
            nc.vector.tensor_copy(b2e[:, :], ps[:, 6, 0:D + 1]).then_inc(s_e1, 1)
            dve.wait_ge(s_e1, 1)
            nc.vector.tensor_scalar(b2e[:, D:D + 1], b2e[:, D:D + 1], 1.0, None, ALU.add).then_inc(s_e1, 1)
            dve.wait_ge(s_e1, 2)
            nc.vector.memset(msg[:, :, :], 0.0).then_inc(s_gz, 1)
            dve.wait_ge(s_gz, 1)
            nc.vector.memset(span[:, 1:2], 0.0).then_inc(s_flag, 1)
            dve.wait_ge(s_xt, NB)
            for t in range(NT):
                nc.vector.tensor_tensor(xN[0:rows_of(t), t, :], xN[0:rows_of(t), t, :], b2e[0:rows_of(t), 0:D],
                                        ALU.add).then_inc(s_xb, 1)
            dve.wait_ge(s_xs, NB)
            flag = dve.value_load(wide[0:1, 0:1], min_val=0, max_val=1)
            with dve.If(flag != 0):
                dc = dcol[:, :, :].rearrange("p q k -> p (q k)")
                with dve.Fori(0, G) as g:
                    dve.wait_ge(s_ge, g * 16 + 16)
                    dve.wait_ge(s_gg, g * 32 + 32)
                    for j in range(ROWS):
                        dve.wait_ge(s_gp, g * ROWS + (j + 1))
                        nc.vector.tensor_tensor(msg[:, j, :], ebuf[:, 0, 0, j * D:(j + 1) * D], gbuf[:, 0, j, :],
                                                ALU.add).then_inc(s_gm, 1)
                        for b in range(NB):
                            last = nc.vector.tensor_scalar(hit_all[:, b, :], iota_b[:, :], float(b * BANK),
                                                           dc[:, bass.ds(g * ROWS + j, 1)], ALU.add, ALU.is_equal)
                        dve.wait_ge(s_gm, g * ROWS + (j + 1))
                        last.then_inc(s_gh, 1)
                dve.wait_ge(s_gp, G * ROWS + 2)
                for b in range(NB):
                    v = aggT[:, b * BANK:b * BANK + width(b)]
                    nc.vector.tensor_tensor(v, v, ps[:, b, 0:width(b)], ALU.add).then_inc(s_agg, 1)
            with dve.Else():
                low_c = lowi[:, :, :].rearrange("p q h -> p (q h)")

                def hits(c, a):
                    r = rel[:, bass.ds(c * (CHUNK * ROWS), CHUNK * ROWS)]
                    nc.vector.tensor_tensor(hit[:, a, :, :], iota_w[:, :, :],
                                            r.unsqueeze(2).to_broadcast([P, CHUNK * ROWS, WIN]),
                                            ALU.is_equal).then_inc(s_hit, 1)
                nc.vector.memset(span[:, 2:3], 0.0).then_inc(s_acc, 4)
                hits(0, 0)
                with dve.Fori(0, STEPS) as i:
                    for a in range(2):
                        hits(i * 2 + (a + 1), 1 - a)
                        for k in range(a * CHUNK, (a + 1) * CHUNK):
                            first = dve.value_load(low_c[0:1, bass.ds(i * BODY + k, 1)], min_val=0, max_val=N - 1)
                            dve.wait_ge(s_win, i * BODY + (k + 1))
                            dve.wait_ge(s_acc, i * BODY + (k + 4))
                            v = aggT[:, bass.ds(first, WIN)]
                            nc.vector.tensor_tensor(v, v, ps[:, 4 + k % 4, 0:WIN], ALU.add).then_inc(s_acc, 1)
                dve.wait_ge(s_acc, G + 4)
                nc.vector.memset(span[:, 3:4], 0.0).then_inc(s_agg, NB)
            for b in range(NB):
                for h in range(HH):
                    dve.wait_ge(s_hc, b * HH + h + 1)
                    nc.vector.bn_stats(bst[:, h, b, :], hT[:, h, b * BANK:b * BANK + width(b)]).then_inc(s_lt, 1)
            dve.wait_ge(s_lt, NB * HH)
            for h in range(HH):
                nc.vector.bn_aggr(bag[:, h, :], bst[:, h, :, :].rearrange("p b s -> p (b s)")).then_inc(s_bn, 2)
            dve.wait_ge(s_sd, 1)
            nc.vector.reciprocal(rsd[:, :], sd[:, :]).then_inc(s_sc, 1)
            dve.wait_ge(s_sc, 1)
            nc.vector.tensor_tensor(scl[:, :], rsd[:, :], col[:, 1, :], ALU.mult).then_inc(s_sc, 1)
            dve.wait_ge(s_sc, 2)
            nc.vector.tensor_tensor(ms[:, :], bag[:, :, 0], scl[:, :], ALU.mult).then_inc(s_sc, 1)
            dve.wait_ge(s_sc, 3)
            nc.vector.tensor_tensor(sft[:, :], col[:, 2, :], ms[:, :], ALU.subtract).then_inc(s_sc, 1)
            dve.wait_ge(s_sc, 4)
            for b in range(NB):
                r = rl[:, b % 2, 0:width(b)]
                hb = hT[:, 1, b * BANK:b * BANK + width(b)]
                if b >= 2:
                    dve.wait_ge(s_rv, b - 1)
                nc.vector.tensor_scalar(r, hb, scl[:, 1:2], sft[:, 1:2], ALU.mult, ALU.add).then_inc(s_lt, 1)
                dve.wait_ge(s_lt, NB * HH + b + 1)
                nc.vector.tensor_scalar(hb, r, 0.0, None, ALU.max).then_inc(s_rv, 1)
            dve.wait_ge(s_xb, NT)
            for b in range(NB):
                t0, t1 = 4 * b, min(4 * b + 4, NT)
                r = rows_of(t1 - 1)
                dve.wait_ge(s_y, b + 1)
                nc.vector.tensor_tensor(yN[0:r, t0:t1, :], ps[0:r, b % 4, 0:(t1 - t0) * D].rearrange("p (t d) -> p t d", d=D),
                                        xN[0:r, t0:t1, :], ALU.add).then_inc(s_yc, 1)
                dve.wait_ge(s_yc, b + 1)
                for t in range(t0, t1):
                    nc.vector.bn_stats(lst[0:r, t, :], yN[0:r, t, :]).then_inc(s_lr, 1)
                dve.wait_ge(s_lr, t1 + 2 * b)
                for t in range(t0, t1):
                    nc.vector.bn_aggr(lag[0:r, t, :], lst[0:r, t, :]).then_inc(s_lg, 1)
                dve.wait_ge(s_ls, b + 1)
                nc.vector.reciprocal(lrs[0:r, t0:t1], lsd[0:r, t0:t1]).then_inc(s_lr, 1)
                dve.wait_ge(s_lr, t1 + 2 * b + 1)
                nc.vector.scalar_tensor_tensor(out=lnb[0:r, t0:t1], in0=lag[0:r, t0:t1, 0], scalar=-1.0,
                                               in1=lrs[0:r, t0:t1], op0=ALU.mult, op1=ALU.mult).then_inc(s_lr, 1)
                dve.wait_ge(s_lr, t1 + 2 * b + 2)
                nc.vector.memset(span[:, 1:2], 0.0).then_inc(s_ln, 1)


_INS = ["x", "src", "dst", "edge_attr_128", "L0_gnn_eps", "L0_gnn_W1", "L0_gnn_b1", "L0_gnn_gamma",
        "L0_gnn_beta", "L0_gnn_W2", "L0_gnn_b2"]


def kernel(**inputs):
    import numpy as _np
    import concourse.bacc as _bacc
    from concourse import mybir as _mybir
    from concourse.bass_utils import run_bass_kernel_spmd as _run

    nc = _bacc.Bacc("TRN2", target_bir_lowering=False, num_devices=1)
    arrays, args = {}, []
    for name in _INS:
        a = _np.ascontiguousarray(inputs[name])
        arrays[f"in_{name}_dram"] = a
        args.append(nc.dram_tensor(f"in_{name}_dram", a.shape, _mybir.dt.from_np(a.dtype), kind="ExternalInput").ap())
    out = nc.dram_tensor("out_0_dram", tuple(inputs["x"].shape), _mybir.dt.float32, kind="ExternalOutput").ap()
    gnn_layer(nc, *args, out)
    r = _run(nc, [arrays], core_ids=[0])
    return r.results[0]["out_0_dram"]
```

```python
from contextlib import ExitStack

import concourse.bass as bass
from concourse import mybir

ALU = mybir.AluOpType
ACT = mybir.ActivationFunctionType
AX_X = mybir.AxisListType.X
F32 = mybir.dt.float32
F16 = mybir.dt.float16
BF16 = mybir.dt.bfloat16
I32 = mybir.dt.int32
U32 = mybir.dt.uint32


P = 128
BANK = 512
LN_EPS = 1e-5
BN_EPS = 1e-5
ROWS = 2
GROUP = P * ROWS
WIN = 20
CHUNK = 3
STEPS_A = 15
A_C = 6
A_G = 6
B_G = 5
RING = 4
RING_C = 3
SPARE = 120
PAD = 8192
PARTS = 3


def gnn_layer(nc, x, src, dst, edge, eps, w1, b1, gamma, beta, w2, b2, out):
    N, D = x.shape
    E = src.shape[0]
    H = w1.shape[1]
    HH = H // P
    NT = -(-N // P)
    NL = N - (NT - 1) * P
    NB = -(-N // BANK)
    Q = -(-E // (2 * GROUP))
    QW = 2 * GROUP
    QL = E - (Q - 1) * QW
    G = 2 * Q
    GL = E - (G - 1) * GROUP
    T = G * ROWS
    GC = STEPS_A * A_C
    STEPS_B = NT // B_G
    GF = G - GC - STEPS_A * A_G - NT
    STEP_W = A_C + A_G
    WA = GF
    WB = WA + STEPS_A * STEP_W
    CB = 2 * -(-(GC * GROUP * N // E + SPARE // 2 + WIN) // 8)
    CNT = 4 * CB
    KEYS = NT * WIN
    HJ = 2 * ROWS
    assert D == P and H == HH * P and GL > 0 and Q <= P and 4 * Q <= BANK and QW - QL <= GL
    assert NT % B_G == 0 and GF == CHUNK and WB + NT == G and KEYS <= BANK and CB <= BANK
    assert A_C == A_G == 2 * CHUNK == 2 * RING_C and CHUNK < B_G < A_G and STEP_W % RING == 0 and NT == 4 * (NB - 1) + 1

    def pos_c(m):
        return 2 * m

    def pos_g(k):
        return 2 * k + 1

    def width(b):
        return min(BANK, N - b * BANK)

    def rows_of(t):
        return NL if t == NT - 1 else P

    x_main = x[0:(NT - 1) * P, :].rearrange("(t p) d -> p t d", p=P)
    out_v = out[0:(NT - 1) * P, :].rearrange("(t p) d -> p t d", p=P)

    with ExitStack() as ctx:
        def sb(name, shape, dt=F32):
            return ctx.enter_context(nc.sbuf_tensor(name, shape, dt))

        def sem(name):
            return ctx.enter_context(nc.semaphore(name))

        big = sb("big", [P, NT * CNT // 2])
        at = [0]

        def part(n):
            v = big[:, at[0]:at[0] + n]
            at[0] += n
            assert at[0] <= NT * CNT // 2
            return v
        cnt = big[:, :].bitcast(F16).rearrange("p (t n) -> p t n", t=NT)
        cnt32 = big[:, :].rearrange("p (t n) -> p t n", t=NT)
        hT = part(HH * N).rearrange("p (h n) -> p h n", h=HH)
        yN = part(NT * D).rearrange("p (t d) -> p t d", d=D)
        oN = part(NT * D).rearrange("p (t d) -> p t d", d=D)
        hit_all = part(NB * BANK).rearrange("p (b n) -> p b n", b=NB)
        msg = part(ROWS * D).rearrange("p (j d) -> p j d", d=D)
        at[0] = 0
        srcf, dstf, dstm, keyf, lof = (part(QW)[0:Q, :] for _ in range(5))
        hiq, loq = (part(QW)[0:Q, :].bitcast(I32) for _ in range(2))
        xr = part(NT * D).rearrange("p (t d) -> p t d", d=D)
        at[0] = 0

        xN = sb("xN", [P, NT, D])
        xp = sb("xp", [P, NT, PARTS, D], BF16)
        aggT = sb("aggT", [P, N + WIN])
        w1_sb = sb("w1_sb", [P, H])
        w2_sb = sb("w2_sb", [P, HH, D])
        col = sb("col", [P, 3, HH])
        row = sb("row", [1, D + 1])
        ones = sb("ones", [P, P])
        zeros = sb("zeros", [P, P])
        diff = sb("diff", [P, P])
        ident = sb("ident", [P, P])
        iota_w = sb("iota_w", [P, CHUNK * ROWS, WIN])
        iota_k = sb("iota_k", [P, KEYS], F16)
        iota_b = sb("iota_b", [P, BANK])
        b2e = sb("b2e", [P, D + 1])
        srcq = sb("srcq", [Q, QW], I32)
        dstq = sb("dstq", [Q, QW], I32)
        ends = sb("ends", [Q, 4])
        endd = sb("endd", [Q, 4, Q])
        low = sb("low", [P, G])
        high = sb("high", [P, G])
        lowi = sb("lowi", [P, G], I32)
        gaps = sb("gaps", [P, 3, G])
        most = sb("most", [P, 4])
        bad = sb("bad", [P, 8])
        tick = sb("tick", [P, 4])
        wide = sb("wide", [P, 1], I32)
        dcol = sb("dcol", [P, Q, HJ])
        rel = sb("rel", [P, T + 2 * B_G])
        key = sb("key", [P, T])
        nlo = sb("nlo", [P, Q, HJ])
        srci = sb("srci", [P, Q, HJ], I32)
        idx = sb("idx", [P, 2, CHUNK * ROWS], I32)
        ebuf = sb("ebuf", [P, 2, CHUNK, ROWS * D])
        erest = sb("erest", [P, 2, CHUNK, ROWS * D])
        elast = sb("elast", [P, 2, CHUNK, ROWS * D], BF16)
        egat = sb("egat", [P, A_G, ROWS * D])
        gbuf = sb("gbuf", [P, A_G, ROWS, PARTS * D], BF16)
        grow = sb("grow", [P, ROWS, D])
        hit = sb("hit", [P, 2, CHUNK * ROWS, WIN], BF16)
        hit_g = sb("hit_g", [P, A_G, ROWS, WIN], BF16)
        hit_f = sb("hit_f", [P, A_G, ROWS, WIN])
        hit_k = sb("hit_k", [P, RING_C, ROWS, KEYS], F16)
        far = sb("far", [P, ROWS, P], F16)
        hit_l = sb("hit_l", [P, RING_C, ROWS, P], F16)
        xtab = nc.dram_tensor("x_parts", (NT * P, PARTS * D), BF16, kind="Internal").ap()
        bst = sb("bst", [P, HH, NB, 6])
        bag = sb("bag", [P, HH, 2])
        sd = sb("sd", [P, HH])
        rsd = sb("rsd", [P, HH])
        scl = sb("scl", [P, HH])
        ms = sb("ms", [P, HH])
        sft = sb("sft", [P, HH])
        epsc = sb("epsc", [P, 2])
        rl = sb("rl", [P, 2, BANK])
        lst = sb("lst", [P, NT, 6])
        lag = sb("lag", [P, NT, 2])
        lsd = sb("lsd", [P, NT])
        lrs = sb("lrs", [P, NT])
        lnb = sb("lnb", [P, NT])
        warm = sb("warm", [1, 1])

        ps = ctx.enter_context(nc.psum_tensor("ps", [P, 8, BANK], F32))
        SUMS = RING

        s_idx = sem("s_idx")
        s_idx1 = sem("s_idx1")
        s_x = sem("s_x")
        s_xz = sem("s_xz")
        s_w = sem("s_w")
        s_edge0 = sem("s_edge0")
        s_edge1 = sem("s_edge1")
        s_tail = sem("s_tail")
        s_eg0 = sem("s_eg0")
        s_eg1 = sem("s_eg1")
        s_cst = sem("s_cst")
        s_id = sem("s_id")
        s_pad = sem("s_pad")
        s_q = sem("s_q")
        s_qs = sem("s_qs")
        s_end = sem("s_end")
        s_endd = sem("s_endd")
        s_bc = sem("s_bc")
        s_turn = sem("s_turn")
        s_b2e = sem("s_b2e")
        s_e1 = sem("s_e1")
        s_low = sem("s_low")
        s_lowi = sem("s_lowi")
        s_bad = sem("s_bad")
        s_dc = sem("s_dc")
        s_rel = sem("s_rel")
        s_flag = sem("s_flag")
        s_xt = sem("s_xt")
        s_xs = sem("s_xs")
        s_xp = sem("s_xp")
        s_xr = sem("s_xr")
        s_xb = sem("s_xb")
        s_ix = sem("s_ix")
        s_hc = sem("s_hc")
        s_hg = sem("s_hg")
        s_hk = sem("s_hk")
        s_win = sem("s_win")
        s_acc = sem("s_acc")
        s_cw = sem("s_cw")
        s_cc = sem("s_cc")
        s_ca = sem("s_ca")
        s_agg = sem("s_agg")
        s_ge = sem("s_ge")
        s_go = sem("s_go")
        s_gg = sem("s_gg")
        s_gx = sem("s_gx")
        s_gm = sem("s_gm")
        s_gh = sem("s_gh")
        s_gp = sem("s_gp")
        s_gz = sem("s_gz")
        s_h = sem("s_h")
        s_hd = sem("s_hd")
        s_bst = sem("s_bst")
        s_bn = sem("s_bn")
        s_sd = sem("s_sd")
        s_sc = sem("s_sc")
        s_r0 = sem("s_r0")
        s_ra = sem("s_ra")
        s_rt = sem("s_rt")
        s_rv = sem("s_rv")
        s_y = sem("s_y")
        s_yc = sem("s_yc")
        s_lst = sem("s_lst")
        s_lg = sem("s_lg")
        s_ls = sem("s_ls")
        s_lr = sem("s_lr")
        s_ln = sem("s_ln")
        s_o = sem("s_o")
        s_out = sem("s_out")
        s_gat = [sem(f"s_gat{k}") for k in range(A_G)]
        s_tab = sem("s_tab")
        s_far = sem("s_far")
        s_hl = sem("s_hl")
        s_er = sem("s_er")
        s_ec = sem("s_ec")
        s_edge = [s_edge0, s_edge1]
        s_eg = [s_eg0, s_eg1]
        used = [0] * CHUNK + [1] * GF

        def upper(v):
            return v.bitcast(BF16).rearrange("p (c two) -> p c two", two=2)[:, :, 1]

        hi_x = xN[:, :, :].bitcast(BF16).rearrange("p t (d two) -> p t d two", two=2)[:, :, :, 1]
        hi_r = xr.bitcast(BF16).rearrange("p t (d two) -> p t d two", two=2)[:, :, :, 1]
        block = ctx.enter_context(nc.Block())
        edge_g = edge[0:(G - 1) * GROUP, :].rearrange("(g p j) d -> p g (j d)", p=P, j=ROWS)
        tail_r = GL // ROWS
        tail_v = edge[(G - 1) * GROUP:(G - 1) * GROUP + tail_r * ROWS, :].rearrange("(p j) d -> p (j d)", j=ROWS)
        tail_1 = edge[E - 1:E, :]

        @block.sync
        def _(sp):
            sp.dma_start(dstq[0:Q - 1, :], dst[0:(Q - 1) * QW].rearrange("(q c) -> q c", c=QW)).then_inc(s_idx, 16)
            sp.dma_start(dstq[Q - 1:Q, 0:QL], dst[(Q - 1) * QW:E].unsqueeze(0)).then_inc(s_idx, 16)
            sp.dma_start(dstq[Q - 1:Q, QL:QW], dst[E - (QW - QL):E].unsqueeze(0)).then_inc(s_idx, 16)
            sp.wait_ge(s_pad, 1)
            sp.dma_start(srcq[0:Q - 1, :], src[0:(Q - 1) * QW].rearrange("(q c) -> q c", c=QW)).then_inc(s_idx1, 16)
            sp.dma_start(srcq[Q - 1:Q, 0:QL], src[(Q - 1) * QW:E].unsqueeze(0)).then_inc(s_idx1, 16)
            sp.wait_ge(s_xp, PARTS)
            sp.dma_start(xtab.rearrange("(t p) d -> p t d", p=P),
                         xp[:, :, :, :].rearrange("p t k d -> p t (k d)")).then_inc(s_tab, 16)
            sp.wait_ge(s_flag, 1)
            flag = sp.value_load(wide[0:1, 0:1], min_val=0, max_val=1)
            with sp.If(flag != 0):
                def group(g):
                    sp.dma_start(ebuf[:, 0, 0, :], edge_g[:, g, :]).then_inc(s_ge, 16)
                group(0)
                with sp.Fori(1, G - 1) as g:
                    sp.wait_ge(s_gm, g * 2)
                    group(g)
                sp.wait_ge(s_gm, (G - 1) * 2)
                sp.dma_start(ebuf[tail_r:tail_r + 1, 0, 0, 0:D], tail_1).then_inc(s_tail, 16)
                sp.wait_ge(s_tail, 16)
                sp.dma_start(ebuf[0:tail_r, 0, 0, :], tail_v).then_inc(s_ge, 16)
                sp.wait_ge(s_tab, 16)
            with sp.Else():
                def chunk(c, a):
                    sp.dma_start(ebuf[:, a, :, :], edge_g[:, bass.ds(c * CHUNK, CHUNK), :]).then_inc(s_edge[a], 16)

                def gathered(g, k, n, a):
                    sp.dma_start(egat[:, k:k + n, :], edge_g[:, bass.ds(g, n), :]).then_inc(s_eg[a], 16)
                g0 = GC + GF
                chunk(0, 0)
                gathered(GC, CHUNK, GF, 1)
                chunk(1, 1)
                gathered(g0, 0, CHUNK, 0)
                sp.wait_ge(s_win, GF)
                gathered(g0 + CHUNK, CHUNK, CHUNK, 1)
                with sp.Fori(1, STEPS_A) as i:
                    for a in range(2):
                        c_end = WA - STEP_W + pos_c(CHUNK * (a + 1) - 1) + 1
                        g_end = WA - STEP_W + pos_g(CHUNK * (a + 1) - 1) + 1
                        sp.wait_ge(s_win, i * STEP_W + c_end)
                        chunk(i * 2 + a, a)
                        sp.wait_ge(s_win, i * STEP_W + g_end)
                        gathered(i * A_G + (g0 + a * CHUNK), a * CHUNK, CHUNK, a)
                gb = g0 + STEPS_A * A_G
                sp.wait_ge(s_win, WB - STEP_W + pos_g(CHUNK - 1) + 1)
                gathered(gb, 0, CHUNK, 0)
                sp.wait_ge(s_win, WB)
                gathered(gb + CHUNK, CHUNK, B_G - CHUNK, 1)
                with sp.Fori(1, STEPS_B - 1) as i:
                    sp.wait_ge(s_win, i * B_G + (WB - B_G + CHUNK))
                    gathered(i * B_G + gb, 0, CHUNK, 0)
                    sp.wait_ge(s_win, i * B_G + WB)
                    gathered(i * B_G + (gb + CHUNK), CHUNK, B_G - CHUNK, 1)
                sp.wait_ge(s_win, G - 2 * B_G + CHUNK)
                gathered(G - B_G, 0, CHUNK, 0)
                sp.wait_ge(s_win, G - B_G)
                sp.dma_start(egat[tail_r:tail_r + 1, B_G - 1, 0:D], tail_1).then_inc(s_tail, 16)
                sp.dma_start(egat[0:tail_r, B_G - 1, :], tail_v).then_inc(s_tail, 16)
                sp.wait_ge(s_tail, 32)
                gathered(G - B_G + CHUNK, CHUNK, B_G - CHUNK - 1, 1)

        @block.gpsimd
        def _(pool):
            nc.gpsimd.memset(xN[:, NT - 1, :], 0.0).then_inc(s_xz, 1)
            nc.gpsimd.iota(diff[:, :], [[1, P]], base=0, channel_multiplier=-1,
                           allow_small_or_imprecise_dtypes=True).then_inc(s_cst, 1)
            nc.gpsimd.memset(ones[:, :], 1.0).then_inc(s_cst, 1)
            nc.gpsimd.iota(iota_w[:, :, :], [[0, CHUNK * ROWS], [1, WIN]], base=0, channel_multiplier=0,
                           allow_small_or_imprecise_dtypes=True).then_inc(s_cst, 1)
            nc.gpsimd.iota(iota_k[:, :], [[1, KEYS]], base=0, channel_multiplier=0,
                           allow_small_or_imprecise_dtypes=True).then_inc(s_cst, 1)
            nc.gpsimd.iota(iota_b[:, :], [[1, BANK]], base=0, channel_multiplier=0,
                           allow_small_or_imprecise_dtypes=True).then_inc(s_cst, 1)
            pool.wait_ge(s_flag, 1)
            flag = pool.value_load(wide[0:1, 0:1], min_val=0, max_val=1)
            src_c = srci[:, :, :].rearrange("p q k -> p (q k)")

            def gather(to, ix, table):
                pool.sem_inc(s_go, 1)
                return nc.gpsimd.indirect_dma_start(to, None, table, bass.IndirectOffsetOnAxis(ap=ix, axis=0))

            with pool.If(flag != 0):
                with pool.Fori(0, G) as g:
                    pool.wait_ge(s_gm, g * 2)
                    nc.gpsimd.tensor_copy(idx[:, 0, 0:ROWS], src_c[:, bass.ds(g * ROWS, ROWS)]).then_inc(s_gx, 1)
                    pool.wait_ge(s_gx, g + 1)
                    for j in range(ROWS):
                        gather(grow[:, j, :], idx[:, 0, j:j + 1], x[:, :]).then_inc(s_gg, 16)
                    pool.wait_ge(s_gg, g * 32 + 32)
            with pool.Else():
                def stage(g, a, n, count):
                    nc.gpsimd.tensor_copy(idx[:, a, 0:n * ROWS], src_c[:, bass.ds(g * ROWS, n * ROWS)]).then_inc(s_ix, 1)
                    pool.wait_ge(s_ix, count)

                def rows(k, a, m):
                    for j in range(ROWS):
                        gather(gbuf[:, k, j, :], idx[:, a, m * ROWS + j:m * ROWS + j + 1],
                               xtab).then_inc(s_gat[k], 16)

                def landed(i, k, done):
                    pool.wait_ge(s_gat[k], i * (16 * ROWS) + done * 16 * ROWS)

                stage(GC, 1, GF, 1)
                pool.wait_ge(s_tab, 16)
                for k in range(GF):
                    rows(CHUNK + k, 1, k)
                g0 = GC + GF
                stage(g0, 0, CHUNK, 2)
                for k in range(CHUNK):
                    rows(k, 0, k)
                for k in range(GF):
                    landed(0, CHUNK + k, 1)
                stage(g0 + CHUNK, 1, CHUNK, 3)
                for k in range(CHUNK):
                    pool.wait_ge(s_win, k + 1)
                    rows(CHUNK + k, 1, k)
                with pool.Fori(1, STEPS_A) as i:
                    for a in range(2):
                        for k in range(a * CHUNK, (a + 1) * CHUNK):
                            landed(i, k, used[k])
                        stage(i * A_G + (g0 + a * CHUNK), a, CHUNK, i * 2 + (a + 2))
                        for k in range(a * CHUNK, (a + 1) * CHUNK):
                            pool.wait_ge(s_win, i * STEP_W + (WA - STEP_W + pos_g(k) + 1))
                            rows(k, a, k - a * CHUNK)
                gb = g0 + STEPS_A * A_G
                for a, n in ((0, CHUNK), (1, B_G - CHUNK)):
                    for k in range(a * CHUNK, (a + 1) * CHUNK):
                        landed(STEPS_A, k, used[k])
                    stage(gb + a * CHUNK, a, n, 2 * STEPS_A + 2 + a)
                    for k in range(a * CHUNK, a * CHUNK + n):
                        pool.wait_ge(s_win, WB - STEP_W + pos_g(k) + 1)
                        rows(k, a, k - a * CHUNK)
                with pool.Fori(1, STEPS_B) as i:
                    for a, n in ((0, CHUNK), (1, B_G - CHUNK)):
                        for k in range(a * CHUNK, a * CHUNK + n):
                            landed(i, k, used[k] + STEPS_A)
                        stage(i * B_G + (gb + a * CHUNK), a, n, i * 2 + (2 * STEPS_A + 2 + a))
                        for k in range(a * CHUNK, a * CHUNK + n):
                            pool.wait_ge(s_win, i * B_G + (WB - B_G + k + 1))
                            rows(k, a, k - a * CHUNK)
            pool.wait_ge(s_xt, NB)
            pool.wait_ge(s_xp, 1)
            pool.wait_ge(s_xr, 1)
            pool.wait_ge(s_e1, 2)
            nc.gpsimd.tensor_tensor(xN[:, :, :], xN[:, :, :], b2e[:, 0:D].unsqueeze(1).to_broadcast([P, NT, D]),
                                    ALU.add).then_inc(s_xb, 1)

        @block.scalar
        def _(act):
            act.dma_start(xN[:, 0:NT - 1, :], x_main).then_inc(s_x, 16)
            act.wait_ge(s_xz, 1)
            act.dma_start(xN[0:NL, NT - 1, :], x[(NT - 1) * P:N, :]).then_inc(s_x, 16)
            act.dma_start(row[0:1, 0:D], b2.unsqueeze(0)).then_inc(s_w, 16)
            act.dma_start(row[0:1, D:D + 1], eps.unsqueeze(0)).then_inc(s_w, 16)
            act.dma_start(w1_sb[:, :], w1).then_inc(s_w, 16)
            act.dma_start(w2_sb[:, :, :], w2.rearrange("(h p) d -> p h d", p=P)).then_inc(s_w, 16)
            for k, v in enumerate((b1, gamma, beta)):
                act.dma_start(col[:, k, :], v.rearrange("(h p) -> p h", p=P),
                              allow_slow_non_contiguous=True).then_inc(s_w, 16)
            act.wait_ge(s_cst, 2)
            nc.scalar.activation(warm[0:1, 0:1], ones[0:1, 0:1], ACT.Sqrt).then_inc(s_r0, 1)
            act.wait_ge(s_x, 32)
            nc.scalar.activation(xp[:, :, 0, :], hi_x, ACT.Copy).then_inc(s_xp, 1)
            act.wait_ge(s_xr, 1)
            nc.scalar.activation(xp[:, :, 1, :], hi_r, ACT.Copy).then_inc(s_xp, 1)
            act.wait_ge(s_e1, 2)
            for b in range(NB):
                act.wait_ge(s_xt, b + 1)
                nc.scalar.activation(aggT[:, b * BANK:b * BANK + width(b)], ps[:, b % 2, 0:width(b)], ACT.Copy,
                                     scale=b2e[:, D:D + 1]).then_inc(s_xs, 1)
            act.wait_ge(s_flag, 1)
            flag = act.value_load(wide[0:1, 0:1], min_val=0, max_val=1)
            with act.If(flag == 0):
                def places(c, r, made):
                    for j in range(ROWS):
                        if j == 0:
                            act.wait_ge(s_hl, made)
                        last = nc.scalar.activation(far[:, j, :], iota_k[:, 0:P], ACT.Abs,
                                                    bias=nlo_c[:, bass.ds(c * ROWS + j, 1)])
                    last.then_inc(s_far, 1)
                    act.wait_ge(s_far, made)
                    nc.scalar.activation(hit_l[:, r, :, :], far[:, :, :], ACT.Relu, bias=ones[:, 0:1],
                                         scale=-1.0).then_inc(s_hl, 1)

                nlo_c = nlo[:, :, :].rearrange("p q k -> p (q k)")
                act.wait_ge(s_rel, 5)
                act.wait_ge(s_xp, PARTS)
                for c in range(RING_C - 1):
                    places(c, c, c + 1)
                with act.Fori(0, STEPS_A) as i:
                    for m in range(A_C):
                        c_next = i * A_C + (m + RING_C - 1)
                        act.wait_ge(s_cw, i * A_C + (m + RING_C))
                        places(c_next, (m + RING_C - 1) % RING_C, i * A_C + (m + RING_C))
                        first = act.value_load(lowi[0:1, bass.ds(i * A_C + m, 1)], min_val=0, max_val=CNT - WIN)
                        act.wait_ge(s_cw, i * A_C + (m + 1 + RING_C))
                        act.wait_ge(s_cc, i * A_C + (m + 1))
                        nc.scalar.activation(cnt[:, :, bass.ds(first + 1, WIN - 1)],
                                             ps[:, m % RING_C, 0:KEYS].rearrange("p (t n) -> p t n", n=WIN)[:, :, 1:WIN],
                                             ACT.Copy).then_inc(s_cc, 1)
            for b in range(NB):
                for h in range(HH):
                    n = b * HH + h
                    act.wait_ge(s_h, n + 1)
                    nc.scalar.activation(hT[:, h, b * BANK:b * BANK + width(b)], ps[:, n % 4, 0:width(b)],
                                         ACT.Identity, bias=col[:, 0, h:h + 1]).then_inc(s_hd, 1)
            act.wait_ge(s_bn, HH)
            nc.scalar.activation(sd[:, :], bag[:, :, 1], ACT.Sqrt, bias=epsc[:, 0:1]).then_inc(s_sd, 1)
            act.wait_ge(s_sc, 4)
            for b in range(NB):
                hb = hT[:, 0, b * BANK:b * BANK + width(b)]
                nc.scalar.activation(hb, hb, ACT.Relu, scale=scl[:, 0:1], bias=sft[:, 0:1]).then_inc(s_ra, 1)
            for b in range(NB):
                t0, t1 = 4 * b, min(4 * b + 4, NT)
                r = rows_of(t1 - 1)
                act.wait_ge(s_lg, t1)
                nc.scalar.activation(lsd[0:r, t0:t1], lag[0:r, t0:t1, 1], ACT.Sqrt,
                                     bias=epsc[0:r, 1:2]).then_inc(s_ls, 1)
                act.wait_ge(s_ln, b + 1)
                for t in range(t0, t1):
                    nc.scalar.activation(oN[0:r, t, :], yN[0:r, t, :], ACT.Identity, scale=lrs[0:r, t:t + 1],
                                         bias=lnb[0:r, t:t + 1]).then_inc(s_o, 1)
                act.wait_ge(s_o, t1)
                if t1 < NT:
                    act.dma_start(out_v[:, t0:t1, :], oN[:, t0:t1, :]).then_inc(s_out, 16)
                else:
                    act.dma_start(out[(NT - 1) * P:N, :], oN[0:NL, NT - 1, :]).then_inc(s_out, 16)
            act.wait_ge(s_out, 16 * NB)

        @block.tensor
        def _(pe):
            pe.wait_ge(s_cst, 2)
            pe.wait_ge(s_endd, 4)
            nc.tensor.matmul(ps[:, 2, 0:4 * Q], ones[0:Q, :], endd[:, :, :].rearrange("q k r -> q (k r)"),
                             start=True, stop=True).then_inc(s_bc, 1)
            pe.wait_ge(s_id, 1)
            for n, (a, need, count) in enumerate(((srcf, s_qs, 2), (dstm, s_q, 3), (keyf, s_q, 4), (lof, s_qs, 5))):
                pe.wait_ge(need, count)
                v = a.rearrange("q (h p j) -> q h j p", h=2, j=ROWS)
                for k in range(HJ):
                    last = nc.tensor.transpose(ps[:, 3 + n, k * Q:(k + 1) * Q], v[:, k // ROWS, k % ROWS, :],
                                               ident[0:Q, 0:Q])
                last.then_inc(s_turn, 1)
            pe.wait_ge(s_w, 112)
            nc.tensor.matmul(ps[:, 7, 0:D + 1], ones[0:1, :], row[0:1, :], start=True, stop=True).then_inc(s_b2e, 1)
            pe.wait_ge(s_x, 32)
            for b in range(NB):
                if b >= 2:
                    pe.wait_ge(s_xs, b - 1)
                for t in range(4 * b, min(4 * b + 4, NT)):
                    r = rows_of(t)
                    k = (t - 4 * b) * P
                    last = nc.tensor.transpose(ps[:, b % 2, k:k + r], xN[0:r, t, :], ident[0:r, 0:r])
                last.then_inc(s_xt, 1)
            pe.wait_ge(s_flag, 1)
            flag = pe.value_load(wide[0:1, 0:1], min_val=0, max_val=1)
            pe.wait_ge(s_xs, NB)
            pe.wait_ge(s_gz, 1)
            pe.wait_ge(s_rel, 5)
            with pe.If(flag != 0):
                pe.wait_ge(s_cst, 5)
                for b in range(NB):
                    last = nc.tensor.matmul(ps[:, b, :], zeros[:, :], iota_b[:, :], start=True, stop=False,
                                            skip_group_check=True)
                last.then_inc(s_gp, 1)
                with pe.Fori(0, G) as g:
                    for j in range(ROWS):
                        pe.wait_ge(s_gh, g * ROWS + j + 1)
                        for b in range(NB):
                            last = nc.tensor.matmul(ps[:, b, :], msg[:, j, :], hit_all[:, b, :], start=False,
                                                    stop=False, skip_group_check=True)
                        last.then_inc(s_gp, 1)
                for b in range(NB):
                    last = nc.tensor.matmul(ps[:, b, :], zeros[:, :], iota_b[:, :], start=False, stop=True,
                                            skip_group_check=True)
                last.then_inc(s_gp, 1)
                pe.wait_ge(s_agg, NB)
            with pe.Else():
                def edge_parts(v, rows_e, rest, last_part, h, start, stop):
                    for n, e in enumerate((upper(rows_e), upper(rest), last_part)):
                        last = nc.tensor.matmul(v, e, h, start=(start and n == 0), stop=(stop and n == 2))
                    return last

                def gathered(w, bank, k, i, before):
                    pe.wait_ge(s_acc, w + 1)
                    v = ps[:, SUMS + bank, 0:WIN]
                    for j in range(ROWS):
                        d = slice(j * D, (j + 1) * D)
                        nc.tensor.matmul(v, egat[:, k, d], hit_f[:, k, j, :], start=(j == 0), stop=False)
                    pe.wait_ge(s_gat[k], i * (16 * ROWS) + (before + 1) * 16 * ROWS)
                    for j in range(ROWS):
                        for n in range(PARTS):
                            last = nc.tensor.matmul(v, gbuf[:, k, j, n * D:(n + 1) * D], hit_g[:, k, j, :],
                                                    start=False, stop=(j == ROWS - 1 and n == PARTS - 1))
                    last.then_inc(s_win, 1)

                pe.wait_ge(s_hg, 1)
                pe.wait_ge(s_eg[1], 16)
                for k in range(GF):
                    gathered(k, k % RING, CHUNK + k, 0, 0)
                with pe.Fori(0, STEPS_A) as i:
                    for m in range(A_C):
                        a = m // CHUNK
                        if m % CHUNK == 0:
                            pe.wait_ge(s_hc, i * 2 + (a + 1))
                            pe.wait_ge(s_edge[a], i * 16 + 16)
                            pe.wait_ge(s_ec, i * 2 + (a + 1))
                        w = WA + pos_c(m)
                        pe.wait_ge(s_acc, i * STEP_W + (w + 1))
                        v = ps[:, SUMS + w % RING, 0:WIN]
                        for j in range(ROWS):
                            d = slice(j * D, (j + 1) * D)
                            last = edge_parts(v, ebuf[:, a, m % CHUNK, d], erest[:, a, m % CHUNK, d],
                                              elast[:, a, m % CHUNK, d], hit[:, a, (m % CHUNK) * ROWS + j, :],
                                              j == 0, j == ROWS - 1)
                        last.then_inc(s_win, 1)
                        pe.wait_ge(s_hk, i * A_C + (m + 1))
                        pe.wait_ge(s_hl, i * A_C + (m + 2))
                        pe.wait_ge(s_ca, i * A_C + (m + 1))
                        for j in range(ROWS):
                            last = nc.tensor.matmul(ps[:, m % RING_C, 0:KEYS], hit_l[:, m % RING_C, j, :],
                                                    hit_k[:, m % RING_C, j, :], start=(j == 0), stop=(j == ROWS - 1))
                        last.then_inc(s_cw, 1)
                        k = m
                        if k % CHUNK == 0:
                            pe.wait_ge(s_hg, i * 2 + (a + 2))
                            pe.wait_ge(s_eg[a], i * 16 + 16 * (a + 1))
                        w = WA + pos_g(k)
                        gathered(i * STEP_W + w, w % RING, k, i, used[k])
                pe.wait_ge(s_ca, GC + RING_C)
                for b in range(4):
                    nc.tensor.matmul(ps[:, b, 0:CB], zeros[:, 0:P].bitcast(BF16)[:, 0:P], cnt[:, 0, b * CB:(b + 1) * CB],
                                     start=True, stop=False, skip_group_check=True)
                with pe.Fori(0, STEPS_B) as i:
                    for k in range(B_G):
                        for n in range(PARTS):
                            w_ap = xp[:, bass.ds(i * B_G + k, 1), n, :].rearrange("p a d -> p (a d)")
                            for b in range(4):
                                nc.tensor.matmul(ps[:, b, 0:CB], w_ap,
                                                 cnt[:, bass.ds(i * B_G + k, 1), b * CB:(b + 1) * CB].rearrange("p a n -> p (a n)"),
                                                 start=False, stop=False, skip_group_check=True)
                        if k % CHUNK == 0:
                            a = k // CHUNK
                            pe.wait_ge(s_hg, i * 2 + (2 * STEPS_A + 2 + a))
                            pe.wait_ge(s_eg[a], i * 16 + 16 * (STEPS_A + 1 + a))
                        w = WB + k
                        pe.wait_ge(s_acc, i * B_G + (w + 4))
                        gathered(i * B_G + w, k % RING, k, i, used[k] + STEPS_A)
                for b in range(4):
                    last = nc.tensor.matmul(ps[:, b, 0:CB], zeros[:, 0:P].bitcast(BF16)[:, 0:P], cnt[:, 0, b * CB:(b + 1) * CB],
                                            start=False, stop=True, skip_group_check=True)
                last.then_inc(s_cw, 1)
                pe.wait_ge(s_agg, NB)
            for b in range(NB):
                pe.wait_ge(s_agg, b + 1)
                for h in range(HH):
                    n = b * HH + h
                    if n >= 4:
                        pe.wait_ge(s_hd, n - 3)
                    nc.tensor.matmul(ps[:, n % 4, 0:width(b)], w1_sb[:, h * P:(h + 1) * P],
                                     aggT[:, b * BANK:b * BANK + width(b)], start=True, stop=True).then_inc(s_h, 1)
            for b in range(NB):
                pe.wait_ge(s_ra, b + 1)
                pe.wait_ge(s_rv, b + 1)
                if b < 4:
                    pe.wait_ge(s_hd, NB * HH)
                if b >= 4:
                    pe.wait_ge(s_yc, b - 3)
                for t in range(4 * b, min(4 * b + 4, NT)):
                    r = rows_of(t)
                    k = (t - 4 * b) * P
                    for h in range(HH):
                        last = nc.tensor.matmul(ps[0:r, b % 4, k:k + D], hT[:, h, t * P:t * P + r], w2_sb[:, h, :],
                                                start=(h == 0), stop=(h == HH - 1))
                last.then_inc(s_y, 1)

        @block.vector
        def _(dve):
            nc.vector.memset(srcq[:, :], -1).then_inc(s_pad, 1)
            nc.vector.memset(zeros[:, :], 0.0).then_inc(s_gz, 1)
            dve.wait_ge(s_cst, 1)
            nc.vector.tensor_scalar(ident[:, :], diff[:, :], 0.0, None, ALU.is_equal).then_inc(s_id, 1)
            nc.vector.memset(rel[:, T:T + 2 * B_G], -1.0).then_inc(s_rel, 1)
            nc.vector.memset(epsc[:, 0:1], BN_EPS).then_inc(s_id, 1)
            nc.vector.memset(epsc[:, 1:2], LN_EPS).then_inc(s_id, 1)
            nc.vector.memset(aggT[:, N:N + WIN], 0.0).then_inc(s_id, 1)
            dve.wait_ge(s_idx, 48)
            nc.vector.tensor_copy(dstf, dstq[:, :]).then_inc(s_q, 1)
            dve.wait_ge(s_q, 1)
            dv = dstf.rearrange("q (h c) -> q h c", h=2)
            nc.vector.tensor_reduce(ends[:, 0:2], dv, AX_X, ALU.min).then_inc(s_end, 1)
            nc.vector.tensor_reduce(ends[:, 2:4], dv, AX_X, ALU.max).then_inc(s_end, 1)
            dve.wait_ge(s_end, 2)
            dve.wait_ge(s_id, 4)
            for k in range(4):
                nc.vector.tensor_scalar(endd[:, k, :], ident[0:Q, 0:Q], ends[:, k:k + 1], None,
                                        ALU.mult).then_inc(s_endd, 1)
            dve.wait_ge(s_idx1, 32)
            dve.wait_ge(s_pad, 1)
            nc.vector.tensor_copy(keyf, srcq[:, :]).then_inc(s_qs, 1)
            dve.wait_ge(s_qs, 1)
            nc.vector.tensor_scalar(srcf, keyf, 0.0, None, ALU.max).then_inc(s_qs, 1)
            nc.vector.tensor_scalar(dstm, keyf, 0.0, float(PAD), ALU.min, ALU.mult).then_inc(s_q, 1)
            dve.wait_ge(s_q, 2)
            nc.vector.tensor_tensor(dstm, dstm, dstf, ALU.add).then_inc(s_q, 1)
            dve.wait_ge(s_bc, 1)
            bc = ps[:, 2, 0:4 * Q].rearrange("p (k h q) -> p k q h", k=2, h=2)
            nc.vector.tensor_copy(low[:, :].rearrange("p (q h) -> p q h", h=2), bc[:, 0, :, :]).then_inc(s_low, 1)
            nc.vector.tensor_copy(high[:, :].rearrange("p (q h) -> p q h", h=2), bc[:, 1, :, :]).then_inc(s_low, 1)
            dve.wait_ge(s_low, 2)
            nc.vector.tensor_copy(lowi[:, :], low[:, :]).then_inc(s_lowi, 1)
            nc.vector.tensor_tensor(gaps[:, 0, :], high[:, :], low[:, :], ALU.subtract).then_inc(s_low, 1)
            nc.vector.tensor_tensor(gaps[:, 1, 0:G - 1], low[:, 1:G], high[:, 0:G - 1], ALU.subtract).then_inc(s_low, 1)
            nc.vector.tensor_tensor(gaps[:, 2, 0:G - 1], low[:, 1:G], low[:, 0:G - 1], ALU.subtract).then_inc(s_low, 1)
            dve.wait_ge(s_low, 5)
            nc.vector.tensor_reduce(most[:, 0:1], gaps[:, 0, :], AX_X, ALU.max).then_inc(s_low, 1)
            nc.vector.tensor_reduce(most[:, 1:2], gaps[:, 0, :], AX_X, ALU.min).then_inc(s_low, 1)
            nc.vector.tensor_reduce(most[:, 2:3], gaps[:, 1, 0:G - 1], AX_X, ALU.min).then_inc(s_low, 1)
            nc.vector.tensor_reduce(most[:, 3:4], gaps[:, 2, 0:G - 1], AX_X, ALU.max).then_inc(s_low, 1)
            dve.wait_ge(s_low, 9)
            end_c = low[:, GC - 1:GC]
            for k, (v, edge_v, op) in enumerate(((most[:, 0:1], WIN, ALU.is_ge), (most[:, 1:2], 1, ALU.is_lt),
                                                 (most[:, 2:3], 0, ALU.is_lt), (most[:, 3:4], WIN, ALU.is_ge),
                                                 (low[:, 0:1], 1, ALU.is_ge), (end_c, CNT - WIN + 1, ALU.is_ge),
                                                 (end_c, CNT - SPARE - WIN, ALU.is_lt))):
                nc.vector.tensor_scalar(bad[:, k:k + 1], v, float(edge_v), None, op).then_inc(s_bad, 1)
            dve.wait_ge(s_bad, 7)
            nc.vector.tensor_reduce(bad[:, 7:8], bad[:, 0:7], AX_X, ALU.max).then_inc(s_bad, 1)
            dve.wait_ge(s_bad, 8)
            nc.vector.tensor_copy(wide[:, :], bad[:, 7:8]).then_inc(s_bad, 1)
            dve.wait_ge(s_turn, 1)
            nc.vector.tensor_copy(srci[:, :, :], ps[:, 3, 0:T].rearrange("p (k q) -> p q k", q=Q)).then_inc(s_rel, 1)
            dve.wait_ge(s_rel, 2)
            dve.wait_ge(s_bad, 9)
            dve.wait_ge(s_lowi, 1)
            nc.vector.memset(tick[:, 0:1], 0.0).then_inc(s_flag, 1)
            nc.vector.tensor_scalar(hiq, srcq[:, :], 7, None, ALU.arith_shift_right).then_inc(s_qs, 1)
            nc.vector.tensor_scalar(loq, srcq[:, :], P - 1, None, ALU.bitwise_and).then_inc(s_qs, 1)
            dve.wait_ge(s_qs, 4)
            dve.wait_ge(s_q, 3)
            nc.vector.scalar_tensor_tensor(out=keyf, in0=hiq, scalar=float(WIN), in1=dstm,
                                           op0=ALU.mult, op1=ALU.add).then_inc(s_q, 1)
            nc.vector.tensor_copy(lof, loq).then_inc(s_qs, 1)
            low_b = low[:, :].unsqueeze(2).to_broadcast([P, G, ROWS])
            dve.wait_ge(s_turn, 2)
            nc.vector.tensor_copy(dcol[:, :, :], ps[:, 4, 0:T].rearrange("p (k q) -> p q k", q=Q)).then_inc(s_dc, 1)
            dve.wait_ge(s_dc, 1)
            nc.vector.tensor_tensor(rel[:, 0:T].rearrange("p (g j) -> p g j", j=ROWS),
                                    dcol[:, :, :].rearrange("p q (h j) -> p (q h) j", j=ROWS), low_b,
                                    ALU.subtract).then_inc(s_rel, 1)
            dve.wait_ge(s_turn, 3)
            key_v = key[:, :].rearrange("p (q k) -> p q k", k=HJ)
            nc.vector.tensor_copy(key_v, ps[:, 5, 0:T].rearrange("p (k q) -> p q k", q=Q)).then_inc(s_dc, 1)
            dve.wait_ge(s_dc, 2)
            key_v = key[:, :].rearrange("p (g j) -> p g j", j=ROWS)
            nc.vector.tensor_tensor(key_v, key_v, low_b, ALU.subtract).then_inc(s_rel, 1)
            dve.wait_ge(s_turn, 4)
            nc.vector.tensor_scalar(nlo[:, :, :], ps[:, 6, 0:T].rearrange("p (k q) -> p q k", q=Q), -1.0, None,
                                    ALU.mult).then_inc(s_rel, 1)
            dve.wait_ge(s_b2e, 1)
            nc.vector.tensor_copy(b2e[:, :], ps[:, 7, 0:D + 1]).then_inc(s_e1, 1)
            dve.wait_ge(s_e1, 1)
            nc.vector.tensor_scalar(b2e[:, D:D + 1], b2e[:, D:D + 1], 1.0, None, ALU.add).then_inc(s_e1, 1)
            dve.wait_ge(s_x, 32)
            nc.vector.tensor_tensor(xr, xN[:, :, :], hi_x, ALU.subtract).then_inc(s_xr, 1)
            dve.wait_ge(s_xr, 1)
            nc.vector.tensor_tensor(xp[:, :, 2, :], xr, hi_r, ALU.subtract).then_inc(s_xp, 1)
            dve.wait_ge(s_xs, NB)
            dve.wait_ge(s_rel, 5)
            dve.wait_ge(s_xp, PARTS)
            dve.wait_ge(s_cst, 5)
            flag = dve.value_load(wide[0:1, 0:1], min_val=0, max_val=1)
            with dve.If(flag != 0):
                dc = dcol[:, :, :].rearrange("p q k -> p (q k)")
                with dve.Fori(0, G) as g:
                    dve.wait_ge(s_ge, g * 16 + 16)
                    dve.wait_ge(s_gg, g * 32 + 32)
                    for j in range(ROWS):
                        dve.wait_ge(s_gp, g * ROWS + (j + 1))
                        nc.vector.tensor_tensor(msg[:, j, :], ebuf[:, 0, 0, j * D:(j + 1) * D], grow[:, j, :],
                                                ALU.add).then_inc(s_gm, 1)
                        for b in range(NB):
                            last = nc.vector.tensor_scalar(hit_all[:, b, :], iota_b[:, :], float(b * BANK),
                                                           dc[:, bass.ds(g * ROWS + j, 1)], ALU.add, ALU.is_equal)
                        dve.wait_ge(s_gm, g * ROWS + (j + 1))
                        last.then_inc(s_gh, 1)
                dve.wait_ge(s_gp, G * ROWS + 2)
                for b in range(NB):
                    v = aggT[:, b * BANK:b * BANK + width(b)]
                    nc.vector.tensor_tensor(v, v, ps[:, b, 0:width(b)], ALU.add).then_inc(s_agg, 1)
            with dve.Else():
                def hits(g, to, n):
                    r = rel[:, bass.ds(g * ROWS, n * ROWS)]
                    return nc.vector.tensor_tensor(to, iota_w[:, 0:n * ROWS, :],
                                                   r.unsqueeze(2).to_broadcast([P, n * ROWS, WIN]), ALU.is_equal)

                def hits_c(c, a):
                    hits(c * CHUNK, hit[:, a, :, :], CHUNK).then_inc(s_hc, 1)

                def hits_g(g, k, n):
                    hits(g, hit_g[:, k:k + n, :, :].rearrange("p k j n -> p (k j) n"), n)
                    hits(g, hit_f[:, k:k + n, :, :].rearrange("p k j n -> p (k j) n"), n).then_inc(s_hg, 1)

                def hits_k(c, r):
                    for j in range(ROWS):
                        last = nc.vector.tensor_scalar(hit_k[:, r, j, :], iota_k[:, :], key[:, bass.ds(c * ROWS + j, 1)],
                                                       None, ALU.is_equal)
                    last.then_inc(s_hk, 1)

                def flat(v):
                    return v.rearrange("p k d -> p (k d)")

                def rest_c(a, landed):
                    dve.wait_ge(s_edge[a], landed)
                    e = flat(ebuf[:, a, :, :])
                    nc.vector.tensor_tensor(flat(erest[:, a, :, :]), e, upper(e), ALU.subtract).then_inc(s_er, 1)

                def last_c(a, made):
                    e = flat(erest[:, a, :, :])
                    dve.wait_ge(s_er, made)
                    nc.vector.tensor_tensor(flat(elast[:, a, :, :]), e, upper(e), ALU.subtract).then_inc(s_ec, 1)

                def add_window(w, bank, g, most_v=N - 1):
                    first = dve.value_load(lowi[0:1, bass.ds(g, 1)], min_val=0, max_val=most_v)
                    dve.wait_ge(s_win, w + 1)
                    dve.wait_ge(s_acc, w + RING)
                    v = aggT[:, bass.ds(first, WIN)]
                    nc.vector.tensor_tensor(v, v, ps[:, SUMS + bank, 0:WIN], ALU.add).then_inc(s_acc, 1)
                    return first

                def add_first(c, r, first):
                    dve.wait_ge(s_cc, c + 2)
                    v = cnt[:, :, bass.ds(first, 1)]
                    nc.vector.tensor_tensor(v, v, ps[:, r, 0:KEYS].rearrange("p (t n) -> p t n", n=WIN)[:, :, 0:1],
                                            ALU.add).then_inc(s_ca, 1)

                g0 = GC + GF
                gb = g0 + STEPS_A * A_G
                nc.vector.memset(cnt32[:, :, 0:1], 0.0).then_inc(s_ca, RING_C)
                nc.vector.memset(cnt32[:, :, (CNT - SPARE) // 2:CNT // 2], 0.0).then_inc(s_cw, RING_C)
                nc.vector.memset(tick[:, 1:2], 0.0).then_inc(s_acc, RING)
                nc.vector.memset(tick[:, 3:4], 0.0).then_inc(s_cc, 1)
                nc.vector.memset(tick[:, 0:1], 0.0).then_inc(s_hl, 1)
                hits_g(GC, CHUNK, GF)
                hits_c(0, 0)
                rest_c(0, 16)
                last_c(0, 1)
                for c in range(2):
                    hits_k(c, c)
                hits_g(g0, 0, CHUNK)
                hits_c(1, 1)
                for k in range(GF):
                    add_window(k, k % RING, GC + k)
                hits_g(g0 + CHUNK, CHUNK, CHUNK)

                def step_a(i, last_step):
                    firsts = []
                    for m in range(A_C):
                        dve.wait_ge(s_cw, i * A_C + (m + RING_C))
                        hits_k(i * A_C + (m + 2), (m + 2) % RING_C)
                        w = WA + pos_c(m)
                        firsts.append(add_window(i * STEP_W + w, w % RING, i * A_C + m, CNT - WIN))
                        if m == 0:
                            rest_c(1, i * 16 + 16)
                        if m == 1:
                            last_c(1, i * 2 + 2)
                        if m == A_C - 2 and not last_step:
                            rest_c(0, i * 16 + 32)
                        if m == A_C - 1 and not last_step:
                            last_c(0, i * 2 + 3)
                        if m >= 1:
                            add_first(i * A_C + (m - 1), (m - 1) % RING_C, firsts[m - 1])
                        w = WA + pos_g(m)
                        add_window(i * STEP_W + w, w % RING, i * A_G + (g0 + m))
                        if m == CHUNK - 1:
                            hits_c(i * 2 + 2, 0)
                            hits_g(i * A_G + (g0 + A_G), 0, CHUNK)
                    add_first(i * A_C + (A_C - 1), (A_C - 1) % RING_C, firsts[A_C - 1])
                    hits_c(i * 2 + 3, 1)
                    if last_step:
                        hits_g(gb + CHUNK, CHUNK, B_G - CHUNK)
                    else:
                        hits_g(i * A_G + (g0 + A_G + CHUNK), CHUNK, CHUNK)

                with dve.Fori(0, STEPS_A - 1) as i:
                    step_a(i, False)
                step_a(STEPS_A - 1, True)

                def step_b(i, last_step):
                    for k in range(B_G):
                        add_window(i * B_G + (WB + k), k % RING, i * B_G + (gb + k))
                        if k == CHUNK - 1 and not last_step:
                            hits_g(i * B_G + (gb + B_G), 0, CHUNK)
                        if k == B_G - 1 and not last_step:
                            hits_g(i * B_G + (gb + B_G + CHUNK), CHUNK, B_G - CHUNK)

                with dve.Fori(0, STEPS_B - 1) as i:
                    step_b(i, False)
                step_b(STEPS_B - 1, True)
                dve.wait_ge(s_acc, G + RING)
                dve.wait_ge(s_cw, GC + RING_C + 1)
                ready = 0
                for b in range(4):
                    v = aggT[:, b * CB:(b + 1) * CB]
                    last = nc.vector.tensor_tensor(v, v, ps[:, b, 0:CB], ALU.add)
                    blocks = NB if b == 3 else (b + 1) * CB // BANK
                    if blocks > ready:
                        last.then_inc(s_agg, blocks - ready)
                        ready = blocks
            for b in range(NB):
                for h in range(HH):
                    dve.wait_ge(s_hd, b * HH + h + 1)
                    nc.vector.bn_stats(bst[:, h, b, :], hT[:, h, b * BANK:b * BANK + width(b)]).then_inc(s_bst, 1)
            dve.wait_ge(s_bst, NB * HH)
            for h in range(HH):
                nc.vector.bn_aggr(bag[:, h, :], bst[:, h, :, :].rearrange("p b s -> p (b s)")).then_inc(s_bn, 1)
            dve.wait_ge(s_sd, 1)
            nc.vector.reciprocal(rsd[:, :], sd[:, :]).then_inc(s_sc, 1)
            dve.wait_ge(s_sc, 1)
            nc.vector.tensor_tensor(scl[:, :], rsd[:, :], col[:, 1, :], ALU.mult).then_inc(s_sc, 1)
            dve.wait_ge(s_sc, 2)
            nc.vector.tensor_tensor(ms[:, :], bag[:, :, 0], scl[:, :], ALU.mult).then_inc(s_sc, 1)
            dve.wait_ge(s_sc, 3)
            nc.vector.tensor_tensor(sft[:, :], col[:, 2, :], ms[:, :], ALU.subtract).then_inc(s_sc, 1)
            dve.wait_ge(s_sc, 4)
            for b in range(NB):
                r = rl[:, b % 2, 0:width(b)]
                hb = hT[:, 1, b * BANK:b * BANK + width(b)]
                if b >= 2:
                    dve.wait_ge(s_rv, b - 1)
                nc.vector.tensor_scalar(r, hb, scl[:, 1:2], sft[:, 1:2], ALU.mult, ALU.add).then_inc(s_rt, 1)
                dve.wait_ge(s_rt, b + 1)
                nc.vector.tensor_scalar(hb, r, 0.0, None, ALU.max).then_inc(s_rv, 1)
            dve.wait_ge(s_xb, 1)
            for b in range(NB):
                t0, t1 = 4 * b, min(4 * b + 4, NT)
                r = rows_of(t1 - 1)
                dve.wait_ge(s_y, b + 1)
                nc.vector.tensor_tensor(yN[0:r, t0:t1, :], ps[0:r, b % 4, 0:(t1 - t0) * D].rearrange("p (t d) -> p t d", d=D),
                                        xN[0:r, t0:t1, :], ALU.add).then_inc(s_yc, 1)
                dve.wait_ge(s_yc, b + 1)
                for t in range(t0, t1):
                    nc.vector.bn_stats(lst[0:r, t, :], yN[0:r, t, :]).then_inc(s_lr, 1)
                dve.wait_ge(s_lr, t1 + 2 * b)
                for t in range(t0, t1):
                    nc.vector.bn_aggr(lag[0:r, t, :], lst[0:r, t, :]).then_inc(s_lg, 1)
                dve.wait_ge(s_ls, b + 1)
                nc.vector.reciprocal(lrs[0:r, t0:t1], lsd[0:r, t0:t1]).then_inc(s_lr, 1)
                dve.wait_ge(s_lr, t1 + 2 * b + 1)
                nc.vector.scalar_tensor_tensor(out=lnb[0:r, t0:t1], in0=lag[0:r, t0:t1, 0], scalar=-1.0,
                                               in1=lrs[0:r, t0:t1], op0=ALU.mult, op1=ALU.mult).then_inc(s_lr, 1)
                dve.wait_ge(s_lr, t1 + 2 * b + 2)
                nc.vector.memset(tick[:, 2:3], 0.0).then_inc(s_ln, 1)


_INS = ["x", "src", "dst", "edge_attr_128", "L0_gnn_eps", "L0_gnn_W1", "L0_gnn_b1", "L0_gnn_gamma",
        "L0_gnn_beta", "L0_gnn_W2", "L0_gnn_b2"]


def kernel(**inputs):
    import numpy as _np
    import concourse.bacc as _bacc
    from concourse import mybir as _mybir
    from concourse.bass_utils import run_bass_kernel_spmd as _run

    nc = _bacc.Bacc("TRN2", target_bir_lowering=False, num_devices=1)
    arrays, args = {}, []
    for name in _INS:
        a = _np.ascontiguousarray(inputs[name])
        arrays[f"in_{name}_dram"] = a
        args.append(nc.dram_tensor(f"in_{name}_dram", a.shape, _mybir.dt.from_np(a.dtype), kind="ExternalInput").ap())
    out = nc.dram_tensor("out_0_dram", tuple(inputs["x"].shape), _mybir.dt.float32, kind="ExternalOutput").ap()
    gnn_layer(nc, *args, out)
    r = _run(nc, [arrays], core_ids=[0])
    return r.results[0]["out_0_dram"]
```

```python
from contextlib import ExitStack

import concourse.bass as bass
from concourse import mybir

ALU = mybir.AluOpType
ACT = mybir.ActivationFunctionType
AX_X = mybir.AxisListType.X
F32 = mybir.dt.float32
F16 = mybir.dt.float16
BF16 = mybir.dt.bfloat16
I32 = mybir.dt.int32


P = 128
BANK = 512
LN_EPS = 1e-5
BN_EPS = 1e-5
ROWS = 2
GROUP = P * ROWS
WIN = 20
CHUNK = 3
STEPS_A = 12
ORDER = "CCGCGCCGCGCCGCGG"
LAG = 2
A_C = ORDER.count("C")
A_G = ORDER.count("G")
FILLS = ((3, 5), (5, 8), (8, 10), (10, 12))
B_C = 4
HALF = 4
RING = 4
RING_C = 3
SPARE = 72
PAD = 8192
PARTS = 3


def gnn_layer(nc, x, src, dst, edge, eps, w1, b1, gamma, beta, w2, b2, out):
    N, D = x.shape
    E = src.shape[0]
    H = w1.shape[1]
    HH = H // P
    NT = -(-N // P)
    NL = N - (NT - 1) * P
    NB = -(-N // BANK)
    Q = -(-E // (2 * GROUP))
    QW = 2 * GROUP
    QL = E - (Q - 1) * QW
    G = 2 * Q
    GL = E - (G - 1) * GROUP
    T = G * ROWS
    GC = STEPS_A * A_C
    GF = A_G
    CHUNKS = A_C // CHUNK
    STEP_W = A_C + A_G
    WA = GF
    WB = WA + STEPS_A * STEP_W
    GB = GC + GF + STEPS_A * A_G
    TILES = [-(-NT // (hi - lo)) for lo, hi in FILLS]
    NT_C = max(n * (hi - lo) for n, (lo, hi) in zip(TILES, FILLS))
    STARTS = [0] + [2 * ((lo * A_C * GROUP * N // E - SPARE // 2) // 2) for lo, hi in FILLS]
    CNT = 2 * -(-(-(-(GC - 1) * GROUP * N // E) + SPARE // 2 + WIN) // 2)
    SIZES = [hi - lo for lo, hi in zip(STARTS, STARTS[1:] + [CNT])]
    EARLY = list(range(STARTS[-1] // BANK))
    PLAIN = list(range(-(-CNT // BANK), NB - 1))
    BLOCKS = EARLY + PLAIN + list(range(len(EARLY), PLAIN[0])) + [NB - 1]
    LAST = 3
    KEYS = NT * WIN
    HJ = 2 * ROWS
    assert D == P and H == HH * P and GL > 0 and Q <= P and 4 * Q <= BANK and QW - QL <= GL
    assert A_G < G - GB < 2 * HALF + 2 and KEYS <= BANK and max(SIZES) <= BANK and NT == 4 * (NB - 1) + 1
    assert A_C == CHUNKS * CHUNK and A_C % RING_C == 0 and STEP_W % RING == 0 and HALF < A_G and RING_C < RING
    assert STEPS_A % 2 == 0 and ORDER[0] == "C" and CHUNKS > 1
    assert max(TILES) <= STEP_W and FILLS[-1][1] == STEPS_A and NT <= B_C * (G - GB - 1)
    place_c = [p for p in range(STEP_W) if ORDER[p] == "C"]
    place_g = [p for p in range(STEP_W) if ORDER[p] == "G"]

    def halves(n):
        return (0, HALF), (HALF, n)

    def width(b):
        return min(BANK, N - b * BANK)

    def rows_of(t):
        return NL if t == NT - 1 else P

    x_main = x[0:(NT - 1) * P, :].rearrange("(t p) d -> p t d", p=P)
    out_v = out[0:(NT - 1) * P, :].rearrange("(t p) d -> p t d", p=P)

    with ExitStack() as ctx:
        def sb(name, shape, dt=F32):
            return ctx.enter_context(nc.sbuf_tensor(name, shape, dt))

        def sem(name):
            return ctx.enter_context(nc.semaphore(name))

        big = sb("big", [P, NT_C * CNT // 2])
        at = [0]

        def part(n):
            v = big[:, at[0]:at[0] + n]
            at[0] += n
            assert at[0] <= NT_C * CNT // 2
            return v
        cnt = big[:, :].bitcast(F16).rearrange("p (t n) -> p t n", t=NT_C)
        cnt32 = big[:, :].rearrange("p (t n) -> p t n", t=NT_C)
        hT = part(HH * N).rearrange("p (h n) -> p h n", h=HH)
        oN = part(NT * D).rearrange("p (t d) -> p t d", d=D)
        hit_all = part(NB * BANK).rearrange("p (b n) -> p b n", b=NB)
        msg = part(ROWS * D).rearrange("p (j d) -> p j d", d=D)
        grow = part(ROWS * D).rearrange("p (j d) -> p j d", d=D)
        at[0] = 0
        srcf, dstf, dstm, keyf, lof = (part(QW)[0:Q, :] for _ in range(5))
        hiq, loq = (part(QW)[0:Q, :].bitcast(I32) for _ in range(2))
        xr = part(NT * D).rearrange("p (t d) -> p t d", d=D)
        T_SET = -(-at[0] // (CNT // 2))
        at[0] = 0

        xN = sb("xN", [P, NT, D])
        xp = sb("xp", [P, NT_C, PARTS, D], BF16)
        aggT = sb("aggT", [P, N + WIN])
        w1_sb = sb("w1_sb", [P, H])
        w2_sb = sb("w2_sb", [P, HH, D])
        col = sb("col", [P, 3, HH])
        row = sb("row", [1, D + 1])
        ones = sb("ones", [P, P])
        zeros = sb("zeros", [P, P])
        diff = sb("diff", [P, P])
        ident = sb("ident", [P, P])
        iota_w = sb("iota_w", [P, HALF * ROWS, WIN])
        iota_k = sb("iota_k", [P, KEYS], F16)
        iota_b = sb("iota_b", [P, BANK])
        b2e = sb("b2e", [P, D + 1])
        srcq = sb("srcq", [Q, QW], I32)
        dstq = sb("dstq", [Q, QW], I32)
        ends = sb("ends", [Q, 4])
        endd = sb("endd", [Q, 4, Q])
        low = sb("low", [P, G])
        high = sb("high", [P, G])
        lowi = sb("lowi", [P, G], I32)
        firsts_a = sb("firsts_a", [1, (STEPS_A + 1) * STEP_W], I32)
        gaps = sb("gaps", [P, 3, G])
        most = sb("most", [P, 4])
        TESTS = 8 + len(FILLS)
        bad = sb("bad", [P, TESTS + 1])
        tick = sb("tick", [P, 4])
        wide = sb("wide", [P, 1], I32)
        dcol = sb("dcol", [P, Q, HJ])
        rel = sb("rel", [P, T + 2 * HALF])
        key = sb("key", [P, T])
        nlo = sb("nlo", [P, Q, HJ])
        srci = sb("srci", [P, Q, HJ], I32)
        idx = sb("idx", [P, 2, A_G * ROWS], I32)
        ebuf = sb("ebuf", [P, CHUNKS, CHUNK, ROWS * D])
        erest = sb("erest", [P, CHUNKS, CHUNK, ROWS * D])
        elast = sb("elast", [P, CHUNKS, CHUNK, ROWS * D], BF16)
        egat = sb("egat", [P, A_G, ROWS * D])
        hit = sb("hit", [P, CHUNKS, CHUNK * ROWS, WIN], BF16)
        hit_f = sb("hit_f", [P, A_G, ROWS, WIN])
        hit_k = sb("hit_k", [P, RING_C, ROWS, KEYS], F16)
        far = sb("far", [P, RING_C, ROWS, P], F16)
        hit_l = sb("hit_l", [P, RING_C, ROWS, P], F16)
        bst = sb("bst", [P, HH, NB, 6])
        bag = sb("bag", [P, HH, 2])
        sd = sb("sd", [P, HH])
        rsd = sb("rsd", [P, HH])
        scl = sb("scl", [P, HH])
        ms = sb("ms", [P, HH])
        sft = sb("sft", [P, HH])
        epsc = sb("epsc", [P, 2])
        rl = sb("rl", [P, 2, BANK])
        lst = sb("lst", [P, NT, 6])
        lag = sb("lag", [P, NT, 2])
        lsd = sb("lsd", [P, NT])
        lrs = sb("lrs", [P, NT])
        lnb = sb("lnb", [P, NT])
        warm = sb("warm", [1, 1])

        ps = ctx.enter_context(nc.psum_tensor("ps", [P, 8, BANK], F32))
        SUMS = RING

        dst_loaded = sem("dst_loaded")
        src_loaded = sem("src_loaded")
        x_loaded = sem("x_loaded")
        x_padded = sem("x_padded")
        weights_loaded = sem("weights_loaded")
        tail_loaded = sem("tail_loaded")
        constants_made = sem("constants_made")
        ident_made = sem("ident_made")
        src_padded = sem("src_padded")
        dst_rows_made = sem("dst_rows_made")
        src_rows_made = sem("src_rows_made")
        src_clipped = sem("src_clipped")
        ends_found = sem("ends_found")
        ends_spread = sem("ends_spread")
        ends_shared = sem("ends_shared")
        rows_turned = sem("rows_turned")
        b2_shared = sem("b2_shared")
        b2_ready = sem("b2_ready")
        low_steps = sem("low_steps")
        lowi_made = sem("lowi_made")
        firsts_ordered = sem("firsts_ordered")
        tests_made = sem("tests_made")
        turned_copied = sem("turned_copied")
        slots_made = sem("slots_made")
        path_known = sem("path_known")
        x_turned = sem("x_turned")
        x_scaled = sem("x_scaled")
        x_parts_made = sem("x_parts_made")
        pads_zeroed = sem("pads_zeroed")
        x_rest_made = sem("x_rest_made")
        x_b2_added = sem("x_b2_added")
        indices_staged = sem("indices_staged")
        chunk_hits_made = sem("chunk_hits_made")
        half_hits_made = sem("half_hits_made")
        key_hits_made = sem("key_hits_made")
        window_summed = sem("window_summed")
        window_added = sem("window_added")
        counts_made = sem("counts_made")
        counts_stored = sem("counts_stored")
        first_counts_added = sem("first_counts_added")
        sums_complete = sem("sums_complete")
        block_multiplied = sem("block_multiplied")
        block_added = sem("block_added")
        gen_edges_loaded = sem("gen_edges_loaded")
        gather_released = sem("gather_released")
        gen_rows_gathered = sem("gen_rows_gathered")
        gen_indices_staged = sem("gen_indices_staged")
        gen_messages_made = sem("gen_messages_made")
        gen_hits_made = sem("gen_hits_made")
        gen_products_made = sem("gen_products_made")
        zeros_made = sem("zeros_made")
        hidden_made = sem("hidden_made")
        hidden_stored = sem("hidden_stored")
        hidden_stats_made = sem("hidden_stats_made")
        hidden_moments_made = sem("hidden_moments_made")
        deviation_made = sem("deviation_made")
        scale_steps = sem("scale_steps")
        table_warmed = sem("table_warmed")
        relu_half0_made = sem("relu_half0_made")
        half1_scaled = sem("half1_scaled")
        relu_half1_made = sem("relu_half1_made")
        rows_made = sem("rows_made")
        row_stats_made = sem("row_stats_made")
        row_moments_made = sem("row_moments_made")
        row_deviations_made = sem("row_deviations_made")
        row_inverses_made = sem("row_inverses_made")
        row_shifts_made = sem("row_shifts_made")
        rows_normalised = sem("rows_normalised")
        rows_written = sem("rows_written")
        slot_gathered = [sem(f"slot_gathered{k}") for k in range(A_G)]
        distances_made = sem("distances_made")
        place_hits_made = sem("place_hits_made")
        edge_rest_made = sem("edge_rest_made")
        edge_parts_made = sem("edge_parts_made")
        chunk_loaded = [sem(f"chunk_loaded{a}") for a in range(CHUNKS)]
        slot_loaded = [sem(f"slot_loaded{k}") for k in range(A_G)]

        def load_firsts(eng, name, i):
            regs = [eng.alloc_register(f"{name}{n}") for n in range(STEP_W)]
            eng.load(regs, firsts_a[0:1, bass.ds(i * STEP_W, STEP_W)])
            return [nc.snap(r, donate=True, min_val=0, max_val=CNT - WIN if ORDER[(n - LAG) % STEP_W] == "C" else N - 1)
                    for n, r in enumerate(regs)]

        def upper(v):
            return v.bitcast(BF16).rearrange("p (c two) -> p c two", two=2)[:, :, 1]

        hi_x = xN[:, :, :].bitcast(BF16).rearrange("p t (d two) -> p t d two", two=2)[:, :, :, 1]
        hi_r = xr.bitcast(BF16).rearrange("p t (d two) -> p t d two", two=2)[:, :, :, 1]
        block = ctx.enter_context(nc.Block())
        edge_g = edge[0:(G - 1) * GROUP, :].rearrange("(g p j) d -> p g (j d)", p=P, j=ROWS)
        tail_r = GL // ROWS
        tail_v = edge[(G - 1) * GROUP:(G - 1) * GROUP + tail_r * ROWS, :].rearrange("(p j) d -> p (j d)", j=ROWS)
        tail_1 = edge[E - 1:E, :]

        @block.sync
        def _(sp):
            sp.dma_start(dstq[0:Q - 1, :], dst[0:(Q - 1) * QW].rearrange("(q c) -> q c", c=QW)).then_inc(dst_loaded, 16)
            sp.dma_start(dstq[Q - 1:Q, 0:QL], dst[(Q - 1) * QW:E].unsqueeze(0)).then_inc(dst_loaded, 16)
            sp.dma_start(dstq[Q - 1:Q, QL:QW], dst[E - (QW - QL):E].unsqueeze(0)).then_inc(dst_loaded, 16)
            sp.wait_ge(src_padded, 1)
            sp.dma_start(srcq[0:Q - 1, :], src[0:(Q - 1) * QW].rearrange("(q c) -> q c", c=QW)).then_inc(src_loaded, 16)
            sp.dma_start(srcq[Q - 1:Q, 0:QL], src[(Q - 1) * QW:E].unsqueeze(0)).then_inc(src_loaded, 16)

            def chunk(c, a):
                sp.dma_start(ebuf[:, a, :, :], edge_g[:, bass.ds(c * CHUNK, CHUNK), :]).then_inc(chunk_loaded[a], 16)

            def slot(g, k):
                sp.dma_start(egat[:, k, :], edge_g[:, bass.ds(g, 1), :].rearrange("p a c -> p (a c)")
                             ).then_inc(slot_loaded[k], 16)

            for k in range(GF):
                slot(GC + k, k)
            for a in range(CHUNKS):
                chunk(a, a)
            sp.wait_ge(path_known, 1)
            flag = sp.value_load(wide[0:1, 0:1], min_val=0, max_val=1)
            with sp.If(flag != 0):
                def group(g):
                    sp.dma_start(ebuf[:, 0, 0, :], edge_g[:, g, :]).then_inc(gen_edges_loaded, 16)
                for a in range(CHUNKS):
                    sp.wait_ge(chunk_loaded[a], 16)
                for k in range(GF):
                    sp.wait_ge(slot_loaded[k], 16)
                group(0)
                with sp.Fori(1, G - 1) as g:
                    sp.wait_ge(gen_messages_made, g * 2)
                    group(g)
                sp.wait_ge(gen_messages_made, (G - 1) * 2)
                sp.dma_start(ebuf[tail_r:tail_r + 1, 0, 0, 0:D], tail_1).then_inc(tail_loaded, 16)
                sp.wait_ge(tail_loaded, 16)
                sp.dma_start(ebuf[0:tail_r, 0, 0, :], tail_v).then_inc(gen_edges_loaded, 16)
            with sp.Else():
                g0 = GC + GF
                for k in range(GF):
                    sp.wait_ge(window_summed, k + 1)
                    slot(g0 + k, k)
                with sp.Fori(1, STEPS_A) as i:
                    for w in range(STEP_W):
                        if ORDER[w] == "G":
                            k = place_g.index(w)
                            sp.wait_ge(window_summed, i * STEP_W + (WA - STEP_W + w + 1))
                            slot(i * A_G + (g0 + k), k)
                        elif place_c.index(w) % CHUNK == CHUNK - 1:
                            a = place_c.index(w) // CHUNK
                            sp.wait_ge(window_summed, i * STEP_W + (WA - STEP_W + w + 1))
                            chunk(i * CHUNKS + a, a)
                sp.wait_ge(window_summed, WB - STEP_W + place_c[CHUNK - 1] + 1)
                chunk(STEPS_A * CHUNKS, 0)
                for n in range(G - 1 - GB):
                    k = n % A_G
                    sp.wait_ge(window_summed, WB - STEP_W + place_g[k] + 1 if n == k else WB + k + 1)
                    slot(GB + n, k)
                k = (G - 1 - GB) % A_G
                sp.wait_ge(window_summed, WB + k + 1)
                sp.dma_start(egat[tail_r:tail_r + 1, k, 0:D], tail_1).then_inc(tail_loaded, 16)
                sp.dma_start(egat[0:tail_r, k, :], tail_v).then_inc(tail_loaded, 16)
                sp.wait_ge(tail_loaded, 32)
                sp.sem_inc(slot_loaded[k], 16)
            for b in range(NB):
                t0, t1 = 4 * b, min(4 * b + 4, NT)
                sp.wait_ge(rows_normalised, t1)
                if t1 < NT:
                    sp.dma_start(out_v[:, t0:t1, :], oN[:, t0:t1, :]).then_inc(rows_written, 16)
                else:
                    sp.dma_start(out[(NT - 1) * P:N, :], oN[0:NL, NT - 1, :]).then_inc(rows_written, 16)
            sp.wait_ge(rows_written, 16 * NB)

        @block.gpsimd
        def _(pool):
            nc.gpsimd.memset(xN[:, NT - 1, :], 0.0).then_inc(x_padded, 1)
            nc.gpsimd.iota(diff[:, :], [[1, P]], base=0, channel_multiplier=-1,
                           allow_small_or_imprecise_dtypes=True).then_inc(constants_made, 1)
            nc.gpsimd.memset(ones[:, :], 1.0).then_inc(constants_made, 1)
            nc.gpsimd.iota(iota_w[:, :, :], [[0, HALF * ROWS], [1, WIN]], base=0, channel_multiplier=0,
                           allow_small_or_imprecise_dtypes=True).then_inc(constants_made, 1)
            nc.gpsimd.iota(iota_k[:, :], [[1, KEYS]], base=0, channel_multiplier=0,
                           allow_small_or_imprecise_dtypes=True).then_inc(constants_made, 1)
            nc.gpsimd.iota(iota_b[:, :], [[1, BANK]], base=0, channel_multiplier=0,
                           allow_small_or_imprecise_dtypes=True).then_inc(constants_made, 1)
            pool.wait_ge(path_known, 1)
            flag = pool.value_load(wide[0:1, 0:1], min_val=0, max_val=1)
            src_c = srci[:, :, :].rearrange("p q k -> p (q k)")

            def gather(to, ix, op=ALU.bypass):
                pool.sem_inc(gather_released, 1)
                return nc.gpsimd.indirect_dma_start(to, None, x[:, :], bass.IndirectOffsetOnAxis(ap=ix, axis=0),
                                                    compute_op=op)

            with pool.If(flag != 0):
                with pool.Fori(0, G) as g:
                    pool.wait_ge(gen_messages_made, g * 2)
                    nc.gpsimd.tensor_copy(idx[:, 0, 0:ROWS],
                                          src_c[:, bass.ds(g * ROWS, ROWS)]).then_inc(gen_indices_staged, 1)
                    pool.wait_ge(gen_indices_staged, g + 1)
                    for j in range(ROWS):
                        gather(grow[:, j, :], idx[:, 0, j:j + 1]).then_inc(gen_rows_gathered, 16)
                    pool.wait_ge(gen_rows_gathered, g * 32 + 32)
            with pool.Else():
                def fetch(s, a, n):
                    nc.gpsimd.tensor_copy(idx[:, a, 0:n * ROWS],
                                          src_c[:, bass.ds(s * (A_G * ROWS) + GC * ROWS, n * ROWS)]
                                          ).then_inc(indices_staged, 1)
                    pool.wait_ge(indices_staged, s + 1)
                    for k in range(n):
                        pool.wait_ge(slot_loaded[k], s * 16 + 16)
                        for j in range(ROWS):
                            m = k * ROWS + j
                            gather(egat[:, k, j * D:(j + 1) * D], idx[:, a, m:m + 1],
                                   ALU.add).then_inc(slot_gathered[k], 16)

                def fetched(s):
                    for k in range(A_G):
                        pool.wait_ge(slot_gathered[k], s * (16 * ROWS) + 16 * ROWS)

                for a in range(2):
                    fetch(a, a, A_G)
                with pool.Fori(1, (STEPS_A + 2) // 2) as i:
                    for a in range(2):
                        fetched(i * 2 + (a - 2))
                        fetch(i * 2 + a, a, A_G)
                fetched(STEPS_A)
                fetch(STEPS_A + 2, 0, G - GB - A_G)
            pool.wait_ge(x_turned, NB)
            pool.wait_ge(x_parts_made, 1)
            pool.wait_ge(x_rest_made, 1)
            pool.wait_ge(b2_ready, 2)
            nc.gpsimd.tensor_tensor(xN[:, :, :], xN[:, :, :], b2e[:, 0:D].unsqueeze(1).to_broadcast([P, NT, D]),
                                    ALU.add).then_inc(x_b2_added, 1)

        @block.scalar
        def _(act):
            act.dma_start(xN[:, 0:NT - 1, :], x_main).then_inc(x_loaded, 16)
            act.wait_ge(x_padded, 1)
            act.dma_start(xN[0:NL, NT - 1, :], x[(NT - 1) * P:N, :]).then_inc(x_loaded, 16)
            act.dma_start(row[0:1, 0:D], b2.unsqueeze(0)).then_inc(weights_loaded, 16)
            act.dma_start(row[0:1, D:D + 1], eps.unsqueeze(0)).then_inc(weights_loaded, 16)
            act.dma_start(w1_sb[:, :], w1).then_inc(weights_loaded, 16)
            act.dma_start(w2_sb[:, :, :], w2.rearrange("(h p) d -> p h d", p=P)).then_inc(weights_loaded, 16)
            for k, v in enumerate((b1, gamma, beta)):
                act.dma_start(col[:, k, :], v.rearrange("(h p) -> p h", p=P),
                              allow_slow_non_contiguous=True).then_inc(weights_loaded, 16)
            act.wait_ge(constants_made, 2)
            nc.scalar.activation(warm[0:1, 0:1], ones[0:1, 0:1], ACT.Sqrt).then_inc(table_warmed, 1)
            act.wait_ge(src_loaded, 32)
            act.wait_ge(src_padded, 1)
            nc.scalar.activation(srcf, srcq[:, :], ACT.Relu).then_inc(src_clipped, 1)
            nc.scalar.activation(dstm, srcq[:, :], ACT.Relu, scale=-1.0).then_inc(src_clipped, 1)
            act.wait_ge(x_loaded, 32)
            nc.scalar.activation(xp[:, 0:NT, 0, :], hi_x, ACT.Copy).then_inc(x_parts_made, 1)
            act.wait_ge(b2_ready, 2)
            for b in range(NB):
                act.wait_ge(x_turned, b + 1)
                nc.scalar.activation(aggT[:, b * BANK:b * BANK + width(b)], ps[:, b % 2, 0:width(b)], ACT.Copy,
                                     scale=b2e[:, D:D + 1]).then_inc(x_scaled, 1)
            act.wait_ge(x_rest_made, 1)
            nc.scalar.activation(xp[:, 0:NT, 1, :], hi_r, ACT.Copy).then_inc(x_parts_made, 1)
            act.wait_ge(path_known, 1)
            flag = act.value_load(wide[0:1, 0:1], min_val=0, max_val=1)
            with act.If(flag == 0):
                def distances(c, r):
                    for j in range(ROWS):
                        last = nc.scalar.activation(far[:, r, j, :], iota_k[:, 0:P], ACT.Abs,
                                                    bias=nlo_c[:, bass.ds(c * ROWS + j, 1)])
                    last.then_inc(distances_made, 1)

                def places(c, r):
                    act.wait_ge(distances_made, c + 1)
                    nc.scalar.activation(hit_l[:, r, :, :], far[:, r, :, :], ACT.Relu, bias=ones[:, 0:1],
                                         scale=-1.0).then_inc(place_hits_made, 1)

                def store(i, m, first):
                    act.wait_ge(counts_made, i * A_C + (m + 1 + RING_C))
                    act.wait_ge(counts_stored, i * A_C + (m + 1))
                    nc.scalar.activation(cnt[:, 0:NT, bass.ds(first + 1, WIN - 1)],
                                         ps[:, m % RING_C, 0:KEYS].rearrange("p (t n) -> p t n", n=WIN)[:, :, 1:WIN],
                                         ACT.Copy).then_inc(counts_stored, 1)

                nlo_c = nlo[:, :, :].rearrange("p q k -> p (q k)")
                act.wait_ge(constants_made, 4)
                act.wait_ge(slots_made, 5)
                for c in range(RING_C - 1):
                    distances(c, c)
                act.wait_ge(place_hits_made, 1)
                for c in range(RING_C - 1):
                    places(c, c)
                act.wait_ge(firsts_ordered, STEP_W)
                with act.Fori(0, STEPS_A) as i:
                    for m in range(A_C):
                        c = i * A_C + (m + RING_C - 1)
                        r = (m + RING_C - 1) % RING_C
                        act.wait_ge(place_hits_made, i * A_C + (m + 1))
                        distances(c, r)
                        if m == 0:
                            firsts = load_firsts(act, "first_act", i)
                        else:
                            store(i, m - 1, firsts[place_c[m - 1] + LAG])
                        act.wait_ge(counts_made, i * A_C + (m + RING_C))
                        places(c, r)
                    store(i, A_C - 1, firsts[place_c[A_C - 1] + LAG])
            act.wait_ge(x_parts_made, PARTS)
            for n in range(NB * HH):
                b, h = BLOCKS[n // HH], n % HH
                act.wait_ge(hidden_made, n + 1)
                nc.scalar.activation(hT[:, h, b * BANK:b * BANK + width(b)], ps[:, n % RING_C, 0:width(b)],
                                     ACT.Identity, bias=col[:, 0, h:h + 1]).then_inc(hidden_stored, 1)
            act.wait_ge(hidden_moments_made, HH)
            nc.scalar.activation(sd[:, :], bag[:, :, 1], ACT.Sqrt, bias=epsc[:, 0:1]).then_inc(deviation_made, 1)
            act.wait_ge(scale_steps, 4)
            for b in range(NB):
                hb = hT[:, 0, b * BANK:b * BANK + width(b)]
                nc.scalar.activation(hb, hb, ACT.Relu, scale=scl[:, 0:1], bias=sft[:, 0:1]).then_inc(relu_half0_made, 1)
            for b in range(NB + 1):
                if b < NB:
                    t0, t1 = 4 * b, min(4 * b + 4, NT)
                    r = rows_of(t1 - 1)
                    act.wait_ge(row_moments_made, t1)
                    nc.scalar.activation(lsd[0:r, t0:t1], lag[0:r, t0:t1, 1], ACT.Sqrt,
                                         bias=epsc[0:r, 1:2]).then_inc(row_deviations_made, 1)
                if b > 0:
                    t0, t1 = 4 * b - 4, min(4 * b, NT)
                    r = rows_of(t1 - 1)
                    act.wait_ge(row_shifts_made, b)
                    for t in range(t0, t1):
                        k = (t - t0) * D
                        nc.scalar.activation(oN[0:r, t, :], ps[0:r, (b + 3) % 8, k:k + D], ACT.Identity,
                                             scale=lrs[0:r, t:t + 1], bias=lnb[0:r, t:t + 1]).then_inc(rows_normalised, 1)

        @block.tensor
        def _(pe):
            pe.wait_ge(constants_made, 2)
            pe.wait_ge(ends_spread, 4)
            nc.tensor.matmul(ps[:, 2, 0:4 * Q], ones[0:Q, :], endd[:, :, :].rearrange("q k r -> q (k r)"),
                             start=True, stop=True).then_inc(ends_shared, 1)
            pe.wait_ge(ident_made, 1)
            turned = ((srcf, src_clipped, 1), (dstm, dst_rows_made, 2), (keyf, dst_rows_made, 3), (lof, src_rows_made, 3))
            for n, (a, need, count) in enumerate(turned):
                pe.wait_ge(need, count)
                v = a.rearrange("q (h p j) -> q h j p", h=2, j=ROWS)
                for k in range(HJ):
                    last = nc.tensor.transpose(ps[:, 3 + n, k * Q:(k + 1) * Q], v[:, k // ROWS, k % ROWS, :],
                                               ident[0:Q, 0:Q])
                last.then_inc(rows_turned, 1)
            pe.wait_ge(weights_loaded, 112)
            nc.tensor.matmul(ps[:, 7, 0:D + 1], ones[0:1, :], row[0:1, :], start=True, stop=True).then_inc(b2_shared, 1)
            pe.wait_ge(x_loaded, 32)
            for b in range(NB):
                if b >= 2:
                    pe.wait_ge(x_scaled, b - 1)
                for t in range(4 * b, min(4 * b + 4, NT)):
                    r = rows_of(t)
                    k = (t - 4 * b) * P
                    last = nc.tensor.transpose(ps[:, b % 2, k:k + r], xN[0:r, t, :], ident[0:r, 0:r])
                last.then_inc(x_turned, 1)
            pe.wait_ge(path_known, 1)
            flag = pe.value_load(wide[0:1, 0:1], min_val=0, max_val=1)
            pe.wait_ge(x_scaled, NB)
            pe.wait_ge(zeros_made, 1)
            pe.wait_ge(slots_made, 5)
            FIRST_H = len(EARLY) * HH

            def hidden(n0, n1):
                for n in range(n0, n1):
                    b, h = BLOCKS[n // HH], n % HH
                    pe.wait_ge(sums_complete, n // HH + 1)
                    if n >= RING_C:
                        pe.wait_ge(hidden_stored, n - RING_C + 1)
                    nc.tensor.matmul(ps[:, n % RING_C, 0:width(b)], w1_sb[:, h * P:(h + 1) * P],
                                     aggT[:, b * BANK:b * BANK + width(b)], start=True,
                                     stop=True).then_inc(hidden_made, 1)

            with pe.If(flag != 0):
                pe.wait_ge(constants_made, 5)
                for b in range(NB):
                    last = nc.tensor.matmul(ps[:, b, :], zeros[:, :], iota_b[:, :], start=True, stop=False,
                                            skip_group_check=True)
                last.then_inc(gen_products_made, 1)
                with pe.Fori(0, G) as g:
                    for j in range(ROWS):
                        pe.wait_ge(gen_hits_made, g * ROWS + j + 1)
                        for b in range(NB):
                            last = nc.tensor.matmul(ps[:, b, :], msg[:, j, :], hit_all[:, b, :], start=False,
                                                    stop=False, skip_group_check=True)
                        last.then_inc(gen_products_made, 1)
                for b in range(NB):
                    last = nc.tensor.matmul(ps[:, b, :], zeros[:, :], iota_b[:, :], start=False, stop=True,
                                            skip_group_check=True)
                last.then_inc(gen_products_made, 1)
                pe.wait_ge(sums_complete, NB)
                hidden(0, FIRST_H)
            with pe.Else():
                def gathered(w, bank, k, landed):
                    pe.wait_ge(window_added, w + 1)
                    pe.wait_ge(slot_gathered[k], landed)
                    for j in range(ROWS):
                        last = nc.tensor.matmul(ps[:, SUMS + bank, 0:WIN], egat[:, k, j * D:(j + 1) * D],
                                                hit_f[:, k, j, :], start=(j == 0), stop=(j == ROWS - 1))
                    last.then_inc(window_summed, 1)

                def multiply(t, f, first=False, done=False):
                    for n in range(PARTS):
                        last = nc.tensor.matmul(ps[:, RING_C, 0:SIZES[f]],
                                                xp[:, bass.ds(t, 1), n, :].rearrange("p a d -> p (a d)"),
                                                cnt[:, bass.ds(t, 1), STARTS[f]:STARTS[f] + SIZES[f]
                                                    ].rearrange("p a n -> p (a n)"),
                                                start=(first and n == 0), stop=(done and n == PARTS - 1),
                                                skip_group_check=True)
                    if done:
                        last.then_inc(block_multiplied, 1)

                for k in range(GF):
                    if k % HALF == 0:
                        pe.wait_ge(half_hits_made, k // HALF + 1)
                    gathered(k, k % RING, k, 16 * ROWS)

                def step_a(i, f=None, first=False):
                    for w in range(STEP_W):
                        n = i * STEP_W + (WA + w)
                        bank = (WA + w) % RING
                        t = -1 if f is None else w - STEP_W + TILES[f] if first else w
                        if first and t == 0:
                            pe.wait_ge(first_counts_added, i * A_C + RING_C)
                            if f:
                                pe.wait_ge(block_added, f)
                        if f is not None and 0 <= t < TILES[f]:
                            multiply(i * TILES[f] + (t - FILLS[f][0] * TILES[f]), f, first and t == 0,
                                     t == TILES[f] - 1)
                        if ORDER[w] == "G":
                            k = place_g.index(w)
                            if k % HALF == 0:
                                pe.wait_ge(half_hits_made, i * 2 + (k // HALF + 3))
                            gathered(n, bank, k, i * (16 * ROWS) + 2 * 16 * ROWS)
                            continue
                        m = place_c.index(w)
                        a = m // CHUNK
                        if m % CHUNK == 0:
                            pe.wait_ge(chunk_hits_made, i * CHUNKS + (a + 1))
                            pe.wait_ge(edge_parts_made, i * CHUNKS + (a + 1))
                            pe.wait_ge(chunk_loaded[a], i * 16 + 16)
                        pe.wait_ge(window_added, n + 1)
                        for j in range(ROWS):
                            d = slice(j * D, (j + 1) * D)
                            parts = (upper(ebuf[:, a, m % CHUNK, d]), upper(erest[:, a, m % CHUNK, d]),
                                     elast[:, a, m % CHUNK, d])
                            for q, e in enumerate(parts):
                                last = nc.tensor.matmul(ps[:, SUMS + bank, 0:WIN], e, hit[:, a, (m % CHUNK) * ROWS + j, :],
                                                        start=(j == 0 and q == 0),
                                                        stop=(j == ROWS - 1 and q == PARTS - 1))
                        last.then_inc(window_summed, 1)
                        pe.wait_ge(key_hits_made, i * A_C + (m + 1))
                        pe.wait_ge(place_hits_made, i * A_C + (m + 2))
                        pe.wait_ge(first_counts_added, i * A_C + (m + 1))
                        for j in range(ROWS):
                            last = nc.tensor.matmul(ps[:, m % RING_C, 0:KEYS], hit_l[:, m % RING_C, j, :],
                                                    hit_k[:, m % RING_C, j, :], start=(j == 0), stop=(j == ROWS - 1))
                        last.then_inc(counts_made, 1)

                with pe.Fori(0, FILLS[0][0]) as i:
                    step_a(i)
                pe.wait_ge(pads_zeroed, 4)
                pe.wait_ge(x_parts_made, PARTS)
                for f, (lo, hi) in enumerate(FILLS):
                    step_a(lo, f, True)
                    with pe.Fori(lo + 1, hi) as i:
                        step_a(i, f)
                for n in range(G - GB):
                    w = WB + n
                    k = n % A_G
                    if n == 1:
                        pe.wait_ge(first_counts_added, GC + RING_C)
                        pe.wait_ge(block_added, len(FILLS))
                    if n > 0:
                        for t in range(min((n - 1) * B_C, NT), min(n * B_C, NT)):
                            multiply(t, len(FILLS), t == 0, t == NT - 1)
                    if n == G - GB - 1:
                        hidden(0, FIRST_H)
                    if k in (0, HALF):
                        pe.wait_ge(half_hits_made, 2 * STEPS_A + 3 + k // HALF + 2 * (n // A_G))
                    gathered(w, w % RING, k, (2 + STEPS_A + n // A_G) * 16 * ROWS)
            hidden(FIRST_H, NB * HH)
            pe.wait_ge(x_b2_added, 1)
            for b in range(NB):
                t0, t1 = 4 * b, min(4 * b + 4, NT)
                r = rows_of(t1 - 1)
                if b == 4:
                    pe.wait_ge(hidden_stored, NB * HH)
                nc.tensor.matmul(ps[0:r, (b + 4) % 8, 0:(t1 - t0) * D], ident[0:r, 0:r],
                                 xN[0:r, t0:t1, :].rearrange("p t d -> p (t d)"), start=True, stop=False,
                                 skip_group_check=True)
            for b in range(NB):
                pe.wait_ge(relu_half0_made, b + 1)
                pe.wait_ge(relu_half1_made, b + 1)
                for t in range(4 * b, min(4 * b + 4, NT)):
                    r = rows_of(t)
                    k = (t - 4 * b) * P
                    for h in range(HH):
                        last = nc.tensor.matmul(ps[0:r, (b + 4) % 8, k:k + D], hT[:, h, t * P:t * P + r], w2_sb[:, h, :],
                                                start=False, stop=(h == HH - 1), skip_group_check=True)
                last.then_inc(rows_made, 1)

        @block.vector
        def _(dve):
            nc.vector.memset(srcq[:, :], -1).then_inc(src_padded, 1)
            nc.vector.memset(zeros[:, :], 0.0).then_inc(zeros_made, 1)
            dve.wait_ge(constants_made, 1)
            nc.vector.tensor_scalar(ident[:, :], diff[:, :], 0.0, None, ALU.is_equal).then_inc(ident_made, 1)
            nc.vector.memset(rel[:, T:T + 2 * HALF], -1.0).then_inc(slots_made, 1)
            nc.vector.memset(epsc[:, 0:1], BN_EPS).then_inc(ident_made, 1)
            nc.vector.memset(epsc[:, 1:2], LN_EPS).then_inc(ident_made, 1)
            nc.vector.memset(aggT[:, N:N + WIN], 0.0).then_inc(ident_made, 1)
            nc.vector.memset(cnt32[:, T_SET:NT, 0:1], 0.0).then_inc(pads_zeroed, 1)
            nc.vector.memset(cnt32[:, T_SET:NT, (CNT - SPARE) // 2:CNT // 2], 0.0).then_inc(pads_zeroed, 1)
            nc.vector.memset(cnt32[:, NT:NT_C, :], 0.0).then_inc(pads_zeroed, 1)
            nc.vector.memset(xp[:, NT:NT_C, :, :], 0.0).then_inc(pads_zeroed, 1)
            dve.wait_ge(dst_loaded, 48)
            nc.vector.tensor_copy(dstf, dstq[:, :]).then_inc(dst_rows_made, 1)
            dve.wait_ge(dst_rows_made, 1)
            dv = dstf.rearrange("q (h c) -> q h c", h=2)
            nc.vector.tensor_reduce(ends[:, 0:2], dv, AX_X, ALU.min).then_inc(ends_found, 1)
            nc.vector.tensor_reduce(ends[:, 2:4], dv, AX_X, ALU.max).then_inc(ends_found, 1)
            dve.wait_ge(ends_found, 2)
            dve.wait_ge(ident_made, 4)
            for k in range(4):
                nc.vector.tensor_scalar(endd[:, k, :], ident[0:Q, 0:Q], ends[:, k:k + 1], None,
                                        ALU.mult).then_inc(ends_spread, 1)
            dve.wait_ge(ends_shared, 1)
            bc = ps[:, 2, 0:4 * Q].rearrange("p (k h q) -> p k q h", k=2, h=2)
            nc.vector.tensor_copy(low[:, :].rearrange("p (q h) -> p q h", h=2), bc[:, 0, :, :]).then_inc(low_steps, 1)
            nc.vector.tensor_copy(high[:, :].rearrange("p (q h) -> p q h", h=2), bc[:, 1, :, :]).then_inc(low_steps, 1)
            dve.wait_ge(low_steps, 2)
            nc.vector.tensor_copy(lowi[:, :], low[:, :]).then_inc(lowi_made, 1)
            nc.vector.tensor_tensor(gaps[:, 0, :], high[:, :], low[:, :], ALU.subtract).then_inc(low_steps, 1)
            nc.vector.tensor_tensor(gaps[:, 1, 0:G - 1], low[:, 1:G], high[:, 0:G - 1],
                                    ALU.subtract).then_inc(low_steps, 1)
            nc.vector.tensor_tensor(gaps[:, 2, 0:G - 1], low[:, 1:G], low[:, 0:G - 1],
                                    ALU.subtract).then_inc(low_steps, 1)
            dve.wait_ge(low_steps, 5)
            nc.vector.tensor_reduce(most[:, 0:1], gaps[:, 0, :], AX_X, ALU.max).then_inc(low_steps, 1)
            nc.vector.tensor_reduce(most[:, 1:2], gaps[:, 0, :], AX_X, ALU.min).then_inc(low_steps, 1)
            nc.vector.tensor_reduce(most[:, 2:3], gaps[:, 1, 0:G - 1], AX_X, ALU.min).then_inc(low_steps, 1)
            nc.vector.tensor_reduce(most[:, 3:4], gaps[:, 2, 0:G - 1], AX_X, ALU.max).then_inc(low_steps, 1)
            dve.wait_ge(low_steps, 9)
            end_c = low[:, GC - 1:GC]
            for k, (v, edge_v, op) in enumerate(((most[:, 0:1], WIN, ALU.is_ge), (most[:, 1:2], 1, ALU.is_lt),
                                                 (most[:, 2:3], 0, ALU.is_lt), (most[:, 3:4], WIN, ALU.is_ge),
                                                 (low[:, 0:1], 1, ALU.is_ge), (end_c, CNT - WIN + 1, ALU.is_ge),
                                                 (end_c, CNT - SPARE - WIN, ALU.is_lt)) + tuple(
                    (low[:, lo * A_C:lo * A_C + 1], STARTS[f + 1], ALU.is_lt) for f, (lo, hi) in enumerate(FILLS)) + (
                    (low[:, G - LAST:G - LAST + 1], (NB - 1) * BANK, ALU.is_lt),)):
                nc.vector.tensor_scalar(bad[:, k:k + 1], v, float(edge_v), None, op).then_inc(tests_made, 1)
            dve.wait_ge(tests_made, TESTS)
            nc.vector.tensor_reduce(bad[:, TESTS:TESTS + 1], bad[:, 0:TESTS], AX_X, ALU.max).then_inc(tests_made, 1)
            dve.wait_ge(tests_made, TESTS + 1)
            nc.vector.tensor_copy(wide[:, :], bad[:, TESTS:TESTS + 1]).then_inc(tests_made, 1)
            dve.wait_ge(rows_turned, 1)
            nc.vector.tensor_copy(srci[:, :, :],
                                  ps[:, 3, 0:T].rearrange("p (k q) -> p q k", q=Q)).then_inc(slots_made, 1)
            dve.wait_ge(slots_made, 2)
            dve.wait_ge(tests_made, TESTS + 2)
            dve.wait_ge(lowi_made, 1)
            nc.vector.memset(tick[:, 0:1], 0.0).then_inc(path_known, 1)
            dve.wait_ge(src_clipped, 2)
            nc.vector.scalar_tensor_tensor(out=dstm, in0=dstm, scalar=float(-PAD), in1=dstf,
                                           op0=ALU.mult, op1=ALU.add).then_inc(dst_rows_made, 1)
            nc.vector.tensor_scalar(hiq, srcq[:, :], 7, None, ALU.arith_shift_right).then_inc(src_rows_made, 1)
            nc.vector.tensor_scalar(loq, srcq[:, :], P - 1, None, ALU.bitwise_and).then_inc(src_rows_made, 1)
            dve.wait_ge(src_rows_made, 2)
            dve.wait_ge(dst_rows_made, 2)
            nc.vector.scalar_tensor_tensor(out=keyf, in0=hiq, scalar=float(WIN), in1=dstm,
                                           op0=ALU.mult, op1=ALU.add).then_inc(dst_rows_made, 1)
            nc.vector.tensor_copy(lof, loq).then_inc(src_rows_made, 1)
            low_b = low[:, :].unsqueeze(2).to_broadcast([P, G, ROWS])
            dve.wait_ge(rows_turned, 2)
            nc.vector.tensor_copy(dcol[:, :, :],
                                  ps[:, 4, 0:T].rearrange("p (k q) -> p q k", q=Q)).then_inc(turned_copied, 1)
            dve.wait_ge(turned_copied, 1)
            nc.vector.tensor_tensor(rel[:, 0:T].rearrange("p (g j) -> p g j", j=ROWS),
                                    dcol[:, :, :].rearrange("p q (h j) -> p (q h) j", j=ROWS), low_b,
                                    ALU.subtract).then_inc(slots_made, 1)
            dve.wait_ge(rows_turned, 3)
            key_v = key[:, :].rearrange("p (q k) -> p q k", k=HJ)
            nc.vector.tensor_copy(key_v, ps[:, 5, 0:T].rearrange("p (k q) -> p q k", q=Q)).then_inc(turned_copied, 1)
            dve.wait_ge(turned_copied, 2)
            key_v = key[:, :].rearrange("p (g j) -> p g j", j=ROWS)
            nc.vector.tensor_tensor(key_v, key_v, low_b, ALU.subtract).then_inc(slots_made, 1)
            dve.wait_ge(rows_turned, 4)
            nc.vector.tensor_scalar(nlo[:, :, :], ps[:, 6, 0:T].rearrange("p (k q) -> p q k", q=Q), -1.0, None,
                                    ALU.mult).then_inc(slots_made, 1)
            dve.wait_ge(b2_shared, 1)
            nc.vector.tensor_copy(b2e[:, :], ps[:, 7, 0:D + 1]).then_inc(b2_ready, 1)
            dve.wait_ge(b2_ready, 1)
            nc.vector.tensor_scalar(b2e[:, D:D + 1], b2e[:, D:D + 1], 1.0, None, ALU.add).then_inc(b2_ready, 1)
            dve.wait_ge(x_loaded, 32)
            nc.vector.tensor_tensor(xr, xN[:, :, :], hi_x, ALU.subtract).then_inc(x_rest_made, 1)
            dve.wait_ge(x_rest_made, 1)
            nc.vector.tensor_tensor(xp[:, 0:NT, 2, :], xr, hi_r, ALU.subtract).then_inc(x_parts_made, 1)
            dve.wait_ge(x_scaled, NB)
            dve.wait_ge(slots_made, 5)
            dve.wait_ge(constants_made, 5)
            flag = dve.value_load(wide[0:1, 0:1], min_val=0, max_val=1)
            with dve.If(flag != 0):
                dc = dcol[:, :, :].rearrange("p q k -> p (q k)")
                with dve.Fori(0, G) as g:
                    dve.wait_ge(gen_edges_loaded, g * 16 + 16)
                    dve.wait_ge(gen_rows_gathered, g * 32 + 32)
                    for j in range(ROWS):
                        dve.wait_ge(gen_products_made, g * ROWS + (j + 1))
                        nc.vector.tensor_tensor(msg[:, j, :], ebuf[:, 0, 0, j * D:(j + 1) * D], grow[:, j, :],
                                                ALU.add).then_inc(gen_messages_made, 1)
                        for b in range(NB):
                            last = nc.vector.tensor_scalar(hit_all[:, b, :], iota_b[:, :], float(b * BANK),
                                                           dc[:, bass.ds(g * ROWS + j, 1)], ALU.add, ALU.is_equal)
                        dve.wait_ge(gen_messages_made, g * ROWS + (j + 1))
                        last.then_inc(gen_hits_made, 1)
                dve.wait_ge(gen_products_made, G * ROWS + 2)
                for b in range(NB):
                    v = aggT[:, b * BANK:b * BANK + width(b)]
                    nc.vector.tensor_tensor(v, v, ps[:, b, 0:width(b)], ALU.add).then_inc(sums_complete, 1)
            with dve.Else():
                def hits(g, to, n):
                    r = rel[:, bass.ds(g * ROWS, n * ROWS)]
                    return nc.vector.tensor_tensor(to, iota_w[:, 0:n * ROWS, :],
                                                   r.unsqueeze(2).to_broadcast([P, n * ROWS, WIN]), ALU.is_equal)

                def hits_c(c, a):
                    hits(c * CHUNK, hit[:, a, :, :], CHUNK).then_inc(chunk_hits_made, 1)

                def hits_g(g, half, n):
                    k0, k1 = halves(n)[half]
                    hits(g + k0, hit_f[:, k0:k1, :, :].rearrange("p k j n -> p (k j) n"),
                         k1 - k0).then_inc(half_hits_made, 1)

                def hits_k(c, r):
                    for j in range(ROWS):
                        last = nc.vector.tensor_scalar(hit_k[:, r, j, :], iota_k[:, :], key[:, bass.ds(c * ROWS + j, 1)],
                                                       None, ALU.is_equal)
                    last.then_inc(key_hits_made, 1)

                def flat(v):
                    return v.rearrange("p k d -> p (k d)")

                def rest_c(a, landed):
                    dve.wait_ge(chunk_loaded[a], landed)
                    e = flat(ebuf[:, a, :, :])
                    nc.vector.tensor_tensor(flat(erest[:, a, :, :]), e, upper(e),
                                            ALU.subtract).then_inc(edge_rest_made, 1)

                def last_c(a, made):
                    e = flat(erest[:, a, :, :])
                    dve.wait_ge(edge_rest_made, made)
                    nc.vector.tensor_tensor(flat(elast[:, a, :, :]), e, upper(e),
                                            ALU.subtract).then_inc(edge_parts_made, 1)

                def add_to(first, w, bank):
                    dve.wait_ge(window_summed, w + 1)
                    dve.wait_ge(window_added, w + RING)
                    v = aggT[:, bass.ds(first, WIN)]
                    nc.vector.tensor_tensor(v, v, ps[:, SUMS + bank, 0:WIN], ALU.add).then_inc(window_added, 1)

                def add_window(w, bank, g):
                    add_to(dve.value_load(lowi[0:1, bass.ds(g, 1)], min_val=0, max_val=N - 1), w, bank)

                def add_first(c, r, first):
                    dve.wait_ge(counts_stored, c + 2)
                    v = cnt[:, 0:NT, bass.ds(first, 1)]
                    nc.vector.tensor_tensor(v, v, ps[:, r, 0:KEYS].rearrange("p (t n) -> p t n", n=WIN)[:, :, 0:1],
                                            ALU.add).then_inc(first_counts_added, 1)

                g0 = GC + GF
                nc.vector.memset(tick[:, 1:2], 0.0).then_inc(window_added, RING)
                for half in range(2):
                    hits_g(GC, half, GF)
                rows_a = firsts_a[:, :].rearrange("p (i w) -> p i w", w=STEP_W)
                for w in range(STEP_W):
                    if ORDER[w] == "C":
                        m = place_c.index(w)
                        to = rows_a[:, 0:STEPS_A, w + LAG]
                        of = lowi[0:1, 0:GC].rearrange("p (i m) -> p i m", m=A_C)[:, :, m]
                    elif w < STEP_W - LAG:
                        k = place_g.index(w)
                        to = rows_a[:, 0:STEPS_A, w + LAG]
                        of = lowi[0:1, g0:GB].rearrange("p (i k) -> p i k", k=A_G)[:, :, k]
                    else:
                        k = place_g.index(w)
                        to = rows_a[:, :, w + LAG - STEP_W]
                        of = lowi[0:1, GC:GB].rearrange("p (i k) -> p i k", k=A_G)[:, :, k]
                    nc.vector.tensor_copy(to, of).then_inc(firsts_ordered, 1)
                nc.vector.memset(tick[:, 0:1], 0.0).then_inc(place_hits_made, 1)
                for k in range(HALF):
                    add_window(k, k % RING, GC + k)
                rest_c(0, 16)
                hits_c(0, 0)
                last_c(0, 1)
                hits_g(g0, 0, A_G)
                dve.wait_ge(firsts_ordered, STEP_W)
                nc.vector.memset(tick[:, 3:4], 0.0).then_inc(counts_stored, 1)
                for c in range(2):
                    hits_k(c, c)
                dve.wait_ge(x_parts_made, PARTS)
                nc.vector.memset(cnt32[:, 0:T_SET, 0:1], 0.0).then_inc(first_counts_added, RING_C)
                nc.vector.memset(cnt32[:, 0:T_SET, (CNT - SPARE) // 2:CNT // 2], 0.0).then_inc(counts_made, RING_C)
                for k in range(HALF, GF - LAG):
                    add_window(k, k % RING, GC + k)

                def add_block(f, done):
                    dve.wait_ge(block_multiplied, sum(hi - lo for lo, hi in FILLS[:f + 1]) + f // len(FILLS))
                    dve.wait_ge(window_added, done)
                    v = aggT[:, STARTS[f]:STARTS[f] + SIZES[f]]
                    nc.vector.tensor_tensor(v, v, ps[:, RING_C, 0:SIZES[f]], ALU.add).then_inc(block_added, 1)

                def step_a(i, name):
                    for w in range(STEP_W):
                        if ORDER[w] == "C":
                            m = place_c.index(w)
                            dve.wait_ge(counts_made, i * A_C + (m + RING_C))
                            hits_k(i * A_C + (m + 2), (m + 2) % RING_C)
                        if w == 0:
                            rest_c(1, i * 16 + 16)
                            firsts = load_firsts(dve, name, i)
                        add_to(firsts[w], i * STEP_W + (WA + w - LAG), (WA + w - LAG) % RING)
                        if w == LAG:
                            hits_g(i * A_G + g0, 1, A_G)
                        if ORDER[w] == "G":
                            k = place_g.index(w)
                            if k == HALF:
                                hits_g(i * A_G + (g0 + A_G), 0, A_G)
                            if w >= STEP_W - LAG:
                                m = A_C + w - STEP_W
                                add_first(i * A_C + m, m % RING_C, firsts[place_c[m] + LAG])
                            continue
                        if m >= LAG:
                            add_first(i * A_C + (m - LAG), (m - LAG) % RING_C, firsts[place_c[m - LAG] + LAG])
                        a = m // CHUNK + 1
                        c = i * CHUNKS + a
                        if m % CHUNK == 0 and m > 0:
                            rest_c(a % CHUNKS, i * 16 + 16 * (1 + a // CHUNKS))
                        if m % CHUNK == 1:
                            last_c(a % CHUNKS, c + 1)
                            hits_c(c, a % CHUNKS)

                steps = [0] + [hi for lo, hi in FILLS]
                for f in range(len(FILLS)):
                    with dve.Fori(steps[f], steps[f + 1]) as i:
                        step_a(i, f"first_dve{f}")
                    add_block(f, steps[f + 1] * STEP_W + WA - LAG + RING)
                dve.wait_ge(block_added, len(FILLS))
                nc.vector.memset(tick[:, 3:4], 0.0).then_inc(sums_complete, len(EARLY))
                for w in range(WB - LAG, G):
                    g = GB + w - WB
                    if w == WB:
                        hits_g(GB, 1, A_G)
                    if w == G - LAST:
                        dve.wait_ge(window_added, w + RING)
                        nc.vector.memset(tick[:, 2:3], 0.0).then_inc(sums_complete, len(PLAIN))
                    if w == G - 1:
                        add_block(len(FILLS), w + RING)
                        dve.wait_ge(block_added, len(FILLS) + 1)
                        nc.vector.memset(tick[:, 0:1], 0.0).then_inc(sums_complete, NB - 1 - len(EARLY) - len(PLAIN))
                    add_window(w, w % RING, g)
                    if w == WB + G - GB - A_G - 1:
                        hits(GB + A_G, hit_f[:, 0:G - GB - A_G, :, :].rearrange("p k j n -> p (k j) n"),
                             G - GB - A_G).then_inc(half_hits_made, 1)
                dve.wait_ge(window_added, G + RING)
                nc.vector.memset(tick[:, 1:2], 0.0).then_inc(sums_complete, 1)
            for n in range(NB * HH):
                b, h = BLOCKS[n // HH], n % HH
                dve.wait_ge(hidden_stored, n + 1)
                nc.vector.bn_stats(bst[:, h, b, :],
                                   hT[:, h, b * BANK:b * BANK + width(b)]).then_inc(hidden_stats_made, 1)
            dve.wait_ge(hidden_stats_made, NB * HH)
            for h in range(HH):
                nc.vector.bn_aggr(bag[:, h, :],
                                  bst[:, h, :, :].rearrange("p b s -> p (b s)")).then_inc(hidden_moments_made, 1)
            dve.wait_ge(deviation_made, 1)
            nc.vector.reciprocal(rsd[:, :], sd[:, :]).then_inc(scale_steps, 1)
            dve.wait_ge(scale_steps, 1)
            nc.vector.tensor_tensor(scl[:, :], rsd[:, :], col[:, 1, :], ALU.mult).then_inc(scale_steps, 1)
            dve.wait_ge(scale_steps, 2)
            nc.vector.tensor_tensor(ms[:, :], bag[:, :, 0], scl[:, :], ALU.mult).then_inc(scale_steps, 1)
            dve.wait_ge(scale_steps, 3)
            nc.vector.tensor_tensor(sft[:, :], col[:, 2, :], ms[:, :], ALU.subtract).then_inc(scale_steps, 1)
            dve.wait_ge(scale_steps, 4)
            for b in range(NB):
                r = rl[:, b % 2, 0:width(b)]
                hb = hT[:, 1, b * BANK:b * BANK + width(b)]
                if b >= 2:
                    dve.wait_ge(relu_half1_made, b - 1)
                nc.vector.tensor_scalar(r, hb, scl[:, 1:2], sft[:, 1:2], ALU.mult, ALU.add).then_inc(half1_scaled, 1)
                dve.wait_ge(half1_scaled, b + 1)
                nc.vector.tensor_scalar(hb, r, 0.0, None, ALU.max).then_inc(relu_half1_made, 1)
            for b in range(NB + 1):
                if b < NB:
                    t0, t1 = 4 * b, min(4 * b + 4, NT)
                    r = rows_of(t1 - 1)
                    dve.wait_ge(rows_made, b + 1)
                    for t in range(t0, t1):
                        k = (t - t0) * D
                        nc.vector.bn_stats(lst[0:r, t, :], ps[0:r, (b + 4) % 8, k:k + D]).then_inc(row_stats_made, 1)
                    dve.wait_ge(row_stats_made, t1)
                    for t in range(t0, t1):
                        nc.vector.bn_aggr(lag[0:r, t, :], lst[0:r, t, :]).then_inc(row_moments_made, 1)
                if b > 0:
                    t0, t1 = 4 * b - 4, min(4 * b, NT)
                    r = rows_of(t1 - 1)
                    dve.wait_ge(row_deviations_made, b)
                    nc.vector.reciprocal(lrs[0:r, t0:t1], lsd[0:r, t0:t1]).then_inc(row_inverses_made, 1)
                    dve.wait_ge(row_inverses_made, b)
                    nc.vector.scalar_tensor_tensor(out=lnb[0:r, t0:t1], in0=lag[0:r, t0:t1, 0], scalar=-1.0,
                                                   in1=lrs[0:r, t0:t1], op0=ALU.mult,
                                                   op1=ALU.mult).then_inc(row_shifts_made, 1)


_INS = ["x", "src", "dst", "edge_attr_128", "L0_gnn_eps", "L0_gnn_W1", "L0_gnn_b1", "L0_gnn_gamma",
        "L0_gnn_beta", "L0_gnn_W2", "L0_gnn_b2"]


def kernel(**inputs):
    import numpy as _np
    import concourse.bacc as _bacc
    from concourse import mybir as _mybir
    from concourse.bass_utils import run_bass_kernel_spmd as _run

    nc = _bacc.Bacc("TRN2", target_bir_lowering=False, num_devices=1)
    arrays, args = {}, []
    for name in _INS:
        a = _np.ascontiguousarray(inputs[name])
        arrays[f"in_{name}_dram"] = a
        args.append(nc.dram_tensor(f"in_{name}_dram", a.shape, _mybir.dt.from_np(a.dtype), kind="ExternalInput").ap())
    out = nc.dram_tensor("out_0_dram", tuple(inputs["x"].shape), _mybir.dt.float32, kind="ExternalOutput").ap()
    gnn_layer(nc, *args, out)
    r = _run(nc, [arrays], core_ids=[0])
    return r.results[0]["out_0_dram"]
```
